# Optimizing a Trainium2 kernel written in Bass

```python
import numpy as np
import jax
import jax.numpy as jnp

def _softmax(x, axis=-1):
    return jax.nn.softmax(x, axis=axis)

def _gelu(x):
    return jax.nn.gelu(x, approximate=True)

def _silu(x):
    return jax.nn.silu(x)

def _sigmoid(x):
    return jax.nn.sigmoid(x)

def _layernorm(x, axis=-1, eps=1e-05):
    m = jnp.mean(x, axis=axis, keepdims=True)
    v = jnp.var(x, axis=axis, keepdims=True)
    return (x - m) / jnp.sqrt(v + eps)

def _scatter_add(tgt, idx, src, axis=0):
    return tgt.at[idx].add(src)

def _segment_sum(src, seg, n):
    return jax.ops.segment_sum(src, seg, n)
kernel_name = 'mk_recurrent_d1_jaxref_r8_94d95e'

def setup_inputs(seed: int=0):
    np.random.seed(seed)
    _w = jnp.asarray

    def _L0_attn_setup():
        import math
        import jax, jax.numpy as jnp
        import numpy as np
        N_HEADS = 16
        N_KV_HEADS = 4
        HEAD_DIM = 128
        D_MODEL = 256
        THETA = 10000.0
        SCALE_BASE = 64

        def _rope_cos_sin(seq_len, head_dim, theta):
            half = head_dim // 2
            inv_freq = 1.0 / theta ** (jnp.arange(half, dtype=jnp.float32) / half)
            pos = jnp.arange(seq_len, dtype=jnp.float32)
            freqs = jnp.outer(pos, inv_freq)
            freqs = jnp.concatenate([freqs, freqs], axis=-1)
            return (jnp.cos(freqs), jnp.sin(freqs))

        def _rotate_half(x):
            half = x.shape[-1] // 2
            return jnp.concatenate([-x[..., half:], x[..., :half]], axis=-1)

        def _xpos_scale(seq_len, head_dim, scale_base):
            pos = jnp.arange(seq_len, dtype=jnp.float32)
            scale = (pos + scale_base / 2.0) / scale_base
            half = head_dim // 2
            s = jnp.broadcast_to(scale[:, None], (seq_len, half))
            return jnp.stack([s, 1.0 / s], axis=-1).reshape(seq_len, head_dim)
        key = jax.random.key(seed)
        ks = jax.random.split(key, 5)
        std = 1.0 / math.sqrt(D_MODEL)
        x = jax.random.normal(ks[0], (2, 256, D_MODEL), dtype=jnp.float32)
        Wq = jax.random.normal(ks[1], (D_MODEL, N_HEADS * HEAD_DIM), dtype=jnp.float32) * std
        Wk = jax.random.normal(ks[2], (D_MODEL, N_KV_HEADS * HEAD_DIM), dtype=jnp.float32) * std
        Wv = jax.random.normal(ks[3], (D_MODEL, N_KV_HEADS * HEAD_DIM), dtype=jnp.float32) * std
        Wo = jax.random.normal(ks[4], (N_HEADS * HEAD_DIM, D_MODEL), dtype=jnp.float32) * std
        return {'x': x, 'Wq': Wq, 'Wk': Wk, 'Wv': Wv, 'Wo': Wo}
    _L0_attn_in = _L0_attn_setup()

    def _L0_ffn_setup():
        import jax, jax.numpy as jnp
        import numpy as np
        H = 256
        I = 176
        E = 16
        K = 2
        SI = I * 2

        def _swiglu(gu, inter):
            g, u = (gu[..., :inter], gu[..., inter:])
            return jax.nn.silu(g) * u
        key = jax.random.key(seed)
        ks = jax.random.split(key, 6)
        s = 0.02
        hidden_states = jax.random.normal(ks[0], (1, 128, H), dtype=jnp.float32)
        gate_w = jax.random.normal(ks[1], (E, H), dtype=jnp.float32) * s
        w_gate_up = jax.random.normal(ks[2], (E, H, 2 * I), dtype=jnp.float32) * s
        w_down = jax.random.normal(ks[3], (E, I, H), dtype=jnp.float32) * s
        shared_gate_up = jax.random.normal(ks[4], (H, 2 * SI), dtype=jnp.float32) * s
        shared_down = jax.random.normal(ks[5], (SI, H), dtype=jnp.float32) * s
        return {'hidden_states': hidden_states, 'gate_w': gate_w, 'w_gate_up': w_gate_up, 'w_down': w_down, 'shared_gate_up': shared_gate_up, 'shared_down': shared_down}
    _L0_ffn_in = _L0_ffn_setup()
    _d = {'L0_attn_x': _L0_attn_in['x'], 'L0_attn_Wq': _L0_attn_in['Wq'], 'L0_attn_Wk': _L0_attn_in['Wk'], 'L0_attn_Wv': _L0_attn_in['Wv'], 'L0_attn_Wo': _L0_attn_in['Wo'], 'L0_ffn_gate_w': _L0_ffn_in['gate_w'], 'L0_ffn_w_gate_up': _L0_ffn_in['w_gate_up'], 'L0_ffn_w_down': _L0_ffn_in['w_down'], 'L0_ffn_shared_gate_up': _L0_ffn_in['shared_gate_up'], 'L0_ffn_shared_down': _L0_ffn_in['shared_down']}
    _x0 = _d['L0_attn_x']
    _d['L0_attn_x'] = jax.random.normal(jax.random.fold_in(jax.random.key(seed), 1), (4, 512, 256), dtype=_x0.dtype)
    del _x0
    return _d

def reference(L0_attn_x, L0_attn_Wq, L0_attn_Wk, L0_attn_Wv, L0_attn_Wo, L0_ffn_gate_w, L0_ffn_w_gate_up, L0_ffn_w_down, L0_ffn_shared_gate_up, L0_ffn_shared_down):

    def _L0_attn_ref(x, Wq, Wk, Wv, Wo):
        import math
        import jax, jax.numpy as jnp
        import numpy as np
        N_HEADS = 16
        N_KV_HEADS = 4
        HEAD_DIM = 128
        D_MODEL = 256
        THETA = 10000.0
        SCALE_BASE = 64

        def _rope_cos_sin(seq_len, head_dim, theta):
            half = head_dim // 2
            inv_freq = 1.0 / theta ** (jnp.arange(half, dtype=jnp.float32) / half)
            pos = jnp.arange(seq_len, dtype=jnp.float32)
            freqs = jnp.outer(pos, inv_freq)
            freqs = jnp.concatenate([freqs, freqs], axis=-1)
            return (jnp.cos(freqs), jnp.sin(freqs))

        def _rotate_half(x):
            half = x.shape[-1] // 2
            return jnp.concatenate([-x[..., half:], x[..., :half]], axis=-1)

        def _xpos_scale(seq_len, head_dim, scale_base):
            pos = jnp.arange(seq_len, dtype=jnp.float32)
            scale = (pos + scale_base / 2.0) / scale_base
            half = head_dim // 2
            s = jnp.broadcast_to(scale[:, None], (seq_len, half))
            return jnp.stack([s, 1.0 / s], axis=-1).reshape(seq_len, head_dim)
        B, S, _ = x.shape
        kv_groups = N_HEADS // N_KV_HEADS
        q = (x @ Wq).reshape(B, S, N_HEADS, HEAD_DIM).transpose(0, 2, 1, 3)
        k = (x @ Wk).reshape(B, S, N_KV_HEADS, HEAD_DIM).transpose(0, 2, 1, 3)
        v = (x @ Wv).reshape(B, S, N_KV_HEADS, HEAD_DIM).transpose(0, 2, 1, 3)
        cos, sin = _rope_cos_sin(S, HEAD_DIM, THETA)
        cos = cos[None, None]
        sin = sin[None, None]
        q = q * cos + _rotate_half(q) * sin
        k = k * cos + _rotate_half(k) * sin
        xscale = _xpos_scale(S, HEAD_DIM, SCALE_BASE)[None, None]
        q = q * xscale
        k = k * (1.0 / xscale)
        k = jnp.repeat(k, kv_groups, axis=1)
        v = jnp.repeat(v, kv_groups, axis=1)
        scale = math.sqrt(HEAD_DIM)
        scores = jnp.einsum('bhqd,bhkd->bhqk', q, k) / scale
        causal = jnp.tril(jnp.ones((S, S), dtype=bool))
        scores = jnp.where(causal[None, None], scores, -jnp.inf)
        attn = jax.nn.softmax(scores, axis=-1)
        out = jnp.einsum('bhqk,bhkd->bhqd', attn, v)
        out = out.transpose(0, 2, 1, 3).reshape(B, S, N_HEADS * HEAD_DIM)
        return out @ Wo

    def _L0_ffn_ref(hidden_states, gate_w, w_gate_up, w_down, shared_gate_up, shared_down):
        import jax, jax.numpy as jnp
        import numpy as np
        H = 256
        I = 176
        E = 16
        K = 2
        SI = I * 2

        def _swiglu(gu, inter):
            g, u = (gu[..., :inter], gu[..., inter:])
            return jax.nn.silu(g) * u
        orig_shape = hidden_states.shape
        x = hidden_states.reshape(-1, H)
        logits = jnp.einsum('th,eh->te', x, gate_w)
        scores = jax.nn.softmax(logits, axis=-1)
        topk_w, topk_idx = jax.lax.top_k(scores, K)
        combine = jnp.sum(jax.nn.one_hot(topk_idx, E, dtype=x.dtype) * topk_w[..., None], axis=1)
        gu = jnp.einsum('th,ehj->etj', x, w_gate_up)
        h = _swiglu(gu, I)
        y = jnp.einsum('eti,eih,te->th', h, w_down, combine)
        gu_s = x @ shared_gate_up
        y = y + _swiglu(gu_s, SI) @ shared_down
        return y.reshape(orig_shape)
    x = L0_attn_x
    xn = _layernorm(x, axis=-1)
    s = _L0_attn_ref(xn, L0_attn_Wq, L0_attn_Wk, L0_attn_Wv, L0_attn_Wo)
    g = _silu(_L0_ffn_ref(xn, L0_ffn_gate_w, L0_ffn_w_gate_up, L0_ffn_w_down, L0_ffn_shared_gate_up, L0_ffn_shared_down))
    x = x + s * g
    return x

_drawn_inputs = setup_inputs


def setup_inputs(seed=0):
    import zlib

    import numpy as np

    out = dict(_drawn_inputs(seed))
    spreads = {}
    factors = {'L0_attn_Wq': 3.037,
     'L0_attn_Wk': 3.048,
     'L0_attn_Wv': 2.925,
     'L0_attn_Wo': 2.897,
     'L0_ffn_gate_w': 8.0,
     'L0_ffn_w_gate_up': 8.0,
     'L0_ffn_w_down': 8.0,
     'L0_ffn_shared_gate_up': 2.915,
     'L0_ffn_shared_down': 2.918}
    for name, (base, spread) in spreads.items():
        noise = np.random.default_rng([zlib.crc32(name.encode()), seed]).standard_normal(out[name].shape)
        drawn = base * np.exp(spread * noise) if base else spread * noise
        out[name] = jnp.asarray(drawn.astype(out[name].dtype))
    for name, factor in factors.items():
        out[name] = (out[name] * factor).astype(out[name].dtype)
    return out
```

```python
from contextlib import ExitStack

import concourse.bass as bass
from concourse import mybir

F32 = mybir.dt.float32
F16 = mybir.dt.float16
BF16 = mybir.dt.bfloat16
U32 = mybir.dt.uint32
ACT = mybir.ActivationFunctionType
ALU = mybir.AluOpType
AX = mybir.AxisListType

P = 128
B, S, D = 4, 512, 256
KC = D // P
TOK = B * S
NT = TOK // P
QT = S // P
NH, NKV, DH = 16, 4, 128
GH = NH // NKV
NG = B * NKV
E_ROUTED, INTER = 16, 176
E_ALL = E_ROUTED + 2
HC = INTER // 2
GU = 2 * INTER
WG, WD = KC * GU, 2 * D
STEPS = E_ALL * NT
EPS = 1e-5

SCORE_UNITS = [[(3, 0)], [(2, 0), (0, 384)], [(1, 0)]]
PT_UNITS = [[(0, 0)], [(1, 0), (3, 384)], [(2, 0)]]
PT_AT = {0: 0, 1: 512, 3: 896, 2: 1024}
PT_UNIT_COLS = [(0, 512), (512, 512), (1024, 256)]
P_AT = [0, 128, 384, 768]
PCOLS = 1280


def build(nc, x, wq, wk, wv, wo, gate_t, w_gate_up, w_down, shared_gu, shared_down, rope, ident, mask, eidx, out):
    with ExitStack() as ctx:
        def sb(name, shape, dt):
            return ctx.enter_context(nc.sbuf_tensor(name, shape, dt))

        def sem(name):
            return ctx.enter_context(nc.semaphore(name))

        ident_f = sb("ident_f", [P, P], F32)
        ident_b = sb("ident_b", [P, P], BF16)
        mask_f = sb("mask_f", [P, P], F32)
        mask_b = sb("mask_b", [P, P], BF16)
        iota_e = sb("iota_e", [P, E_ROUTED], F32)
        tab = sb("tab", [P, 4, S], F32)
        x_sb = sb("x_sb", [P, NT * D], F32)
        s_sb = sb("s_sb", [P, NT * D], F32)
        y_sb = sb("y_sb", [P, NT * D], F32)
        xnT = [sb("xnT_hi", [P, KC * TOK], F16), sb("xnT_lo", [P, KC * TOK], BF16)]
        xn = sb("xn", [P, 4 * D], F32)
        stats = sb("stats", [P, NT, 6], F32)
        mv = sb("mv", [P, NT, 2], F32)
        rstd = sb("rstd", [P, NT], F32)
        var = sb("var", [P, NT], F32)
        root = sb("root", [P, NT], F32)
        logit = sb("logit", [P, NT, E_ROUTED], F32)
        top = sb("top", [P, NT, 8], F32)
        topi = sb("topi", [P, NT, 8], U32)
        topf = sb("topf", [P, NT, 2], F32)
        sel = sb("sel", [P, NT, E_ROUTED], F32)
        sel2 = sb("sel2", [P, NT, E_ROUTED], F32)
        prob = sb("prob", [P, NT, E_ROUTED], F32)
        zsum = sb("zsum", [P, NT], F32)
        one = sb("one", [P, 1], F32)
        comb = sb("comb", [P, E_ALL * NT], F32)
        NSTG = 3
        stage = sb("stage", [P, NSTG, 2048], F32)
        wkv_s = [sb("wkv_hi", [P, 2 * KC * 512], F16), sb("wkv_lo", [P, 2 * KC * 512], BF16)]
        wq_s = [sb("wq_hi", [P, KC * 2048], F16), sb("wq_lo", [P, KC * 2048], BF16)]
        wo_s = [sb("wo_hi", [P, NH * D], F16), sb("wo_lo", [P, NH * D], BF16)]
        gate_s = [sb("gate_hi", [P, KC * E_ROUTED], F16), sb("gate_lo", [P, KC * E_ROUTED], BF16)]
        qT = [sb("qT_hi", [P, GH * S], F16), sb("qT_lo", [P, GH * S], BF16)]
        kT = [sb("kT_hi", [P, S], F16), sb("kT_lo", [P, S], BF16)]
        v_s = [sb("v_hi", [P, S], F16), sb("v_lo", [P, S], BF16)]
        rot_a = [sb(f"rot_a{n}", [P, S], F32) for n in range(3)]
        rot_b = [sb(f"rot_b{n}", [P, S], F32) for n in range(3)]
        probs = [sb(f"probs{n}", [P, PCOLS], F32) for n in range(2)]
        nmax = sb("nmax", [P, 2, QT], F32)
        rsum = sb("rsum", [P, 2, QT], F32)
        rinv = sb("rinv", [P, 2, QT], F32)
        pT = [[sb(f"pT_hi{n}", [P, PCOLS], F16), sb(f"pT_lo{n}", [P, PCOLS], BF16)] for n in range(2)]
        oT = [sb("oT_hi", [P, GH * S], F16), sb("oT_lo", [P, GH * S], BF16)]
        wg_s = [sb("wg_hi", [P, 2 * WG], F16), sb("wg_lo", [P, 2 * WG], BF16)]
        wd_s = [stage[:, 2, 0:WD].bitcast(F16), stage[:, 2, WD:2 * WD].bitcast(BF16)]
        sg = probs[0][:, 0:2 * INTER].rearrange("p (r n) -> p r n", r=2)
        hid = probs[1][:, 0:2 * INTER].rearrange("p (r n) -> p r n", r=2)
        hT = [w[0:HC, 0:8 * P].rearrange("p (r n) -> p r n", r=4) for w in pT[0]]

        bank = [ctx.enter_context(nc.psum_tensor(f"bank{n}", [P, 512], F32)) for n in range(8)]
        score_bank, pt_bank, o_bank, misc_bank = bank[0:3], bank[3:5], bank[5], bank[6:8]
        gu_bank, hT_bank, y_bank = bank[0:2], bank[2:4], bank[4:6]
        xnT_bank, logit_bank = bank[6:8], bank[5]

        x_in, const_in, gate_in = sem("x_in"), sem("const_in"), sem("gate_in")
        stage_in = [sem(f"stage_in{n}") for n in range(5)]
        const_cast, zeroed = sem("const_cast"), sem("zeroed")
        w_hi, w_lo = sem("w_hi"), sem("w_lo")
        ln_step, xn_ready, xnT_ps, xnT_hi, xnT_lo = sem("ln_step"), sem("xn_ready"), sem("xnT_ps"), sem("xnT_hi"), sem("xnT_lo")
        var_ready, rooted, newton = sem("var_ready"), sem("rooted"), sem("newton")
        logit_ps, rt, rt_exp = sem("logit_ps"), sem("rt"), sem("rt_exp")
        scores, maxed, exped, inverted, normed = sem("scores"), sem("maxed"), sem("exped"), sem("inverted"), sem("normed")
        pt_ps, pt_hi, pt_lo = sem("pt_ps"), sem("pt_hi"), sem("pt_lo")
        pv, o_hi, o_lo = sem("pv"), sem("o_hi"), sem("o_lo")
        misc_ps, misc_free = sem("misc_ps"), sem("misc_free")
        rot_add, rot_hi, rot_lo, v_hi = sem("rot_add"), sem("rot_hi"), sem("rot_lo"), sem("v_hi")
        exp_w_in = [sem(f"exp_w_in{n}") for n in range(2)]
        wg_hi, wd_hi, exp_w = sem("wg_hi"), sem("wd_hi"), sem("exp_w")
        gu_ps, silued, hidden, hT_ps, hT_hi, hT_lo, down_ps, y_done = (
            sem("gu_ps"), sem("silued"), sem("hidden"), sem("hT_ps"), sem("hT_hi"), sem("hT_lo"), sem("down_ps"), sem("y_done"))
        gate_act, gated, summed, stored = sem("gate_act"), sem("gated"), sem("summed"), sem("stored")

        PASSES = ((0, 0), (0, 1), (1, 0))

        W_CHUNKS = [(wkv_s, 0, 2048), (wq_s, 0, 2048), (wq_s, 2048, 2048), (wo_s, 0, 2048), (wo_s, 2048, 2048)]
        N_CHUNKS = len(W_CHUNKS)
        ROT = ["q0", "q1", "q2", "k", "q3"]
        ROT_BUF = {"q0": 0, "q1": 1, "q2": 0, "k": 2, "q3": 1}
        PROJ_ITEMS = len(ROT) + 1
        MISC_ROUND = PROJ_ITEMS + 2

        block = ctx.enter_context(nc.Block())

        @block.sync
        def _(sp):
            sp.dma_start(x_sb[:].rearrange("p (t d) -> p t d", d=D), x.rearrange("b (t p) d -> p (b t) d", p=P)).then_inc(x_in, 16)
            sp.dma_start(ident_f[:], ident).then_inc(const_in, 16)
            sp.dma_start(mask_f[:], mask).then_inc(const_in, 16)
            sp.dma_start(iota_e[:], eidx).then_inc(const_in, 16)
            sp.dma_start(tab[:], rope.rearrange("a p s -> p a s")).then_inc(const_in, 16)
            sp.dma_start(stage[:, 0, 0:1024].rearrange("p (c n) -> p c n", c=KC), wk.rearrange("(c p) n -> p c n", p=P)).then_inc(stage_in[0], 16)
            sp.dma_start(stage[:, 0, 1024:2048].rearrange("p (c n) -> p c n", c=KC), wv.rearrange("(c p) n -> p c n", p=P)).then_inc(stage_in[0], 16)
            sp.dma_start(stage[:, 1, :], wq[0:P, :]).then_inc(stage_in[1], 16)
            sp.dma_start(stage[:, 2, :], wq[P:2 * P, :]).then_inc(stage_in[2], 16)
            for half in range(2):
                sp.wait_ge(w_lo, half + 1)
                sp.dma_start(stage[:, half, :].rearrange("p (h n) -> p h n", n=D),
                             wo[half * 1024:(half + 1) * 1024, :].rearrange("(h p) n -> p h n", p=P)).then_inc(stage_in[3 + half], 16)

            def load_expert(e, par):
                sp.dma_start(stage[:, par, 0:WG].rearrange("p (c n) -> p c n", c=KC),
                             w_gate_up[bass.ds(e, 1)].rearrange("o (c p) n -> p (o c) n", p=P)).then_inc(exp_w_in[par], 16)
                sp.dma_start(stage[0:HC, par, WG:WG + WD].rearrange("p (c n) -> p c n", c=2),
                             w_down[bass.ds(e, 1)].rearrange("o (c p) n -> p (o c) n", p=HC)).then_inc(exp_w_in[par], 16)

            def load_shared(half, par):
                for c in range(KC):
                    sp.dma_start(stage[:, par, c * GU:(c + 1) * GU].rearrange("p (w n) -> p w n", w=2),
                                 shared_gu[c * P:(c + 1) * P, :].rearrange("p (w n) -> p w n", w=2)[:, :, half * INTER:(half + 1) * INTER]
                                 ).then_inc(exp_w_in[par], 16)
                sp.dma_start(stage[0:HC, par, WG:WG + WD].rearrange("p (c n) -> p c n", c=2),
                             shared_down[half * INTER:(half + 1) * INTER, :].rearrange("(c p) n -> p c n", p=HC)).then_inc(exp_w_in[par], 16)

            sp.wait_ge(w_lo, N_CHUNKS)
            for e in range(2):
                load_expert(e, e)
            with sp.Fori(1, E_ROUTED // 2) as r:
                for par in range(2):
                    sp.wait_ge(exp_w, r * 2 + par - 1)
                    load_expert(r * 2 + par, par)
            for half in range(2):
                sp.wait_ge(exp_w, E_ROUTED + half - 1)
                load_shared(half, half)
            out_t = out.rearrange("b (t p) d -> p b t d", p=P)
            for b in range(B):
                sp.wait_ge(summed, b + 1)
                sp.dma_start(out_t[:, b], s_sb[:, b * QT * D:(b + 1) * QT * D].rearrange("p (t d) -> p t d", d=D)).then_inc(stored, 16)
            sp.wait_ge(stored, 16 * B)

        @block.gpsimd
        def _(pool):
            pool.memset(s_sb[:], 0.0).then_inc(zeroed, 1)
            pool.memset(y_sb[:], 0.0).then_inc(zeroed, 1)
            pool.memset(one[:], 1.0).then_inc(zeroed, 1)
            pool.memset(comb[:, E_ROUTED * NT:], 1.0).then_inc(zeroed, 1)
            for n, (dst, at, cols) in enumerate(W_CHUNKS):
                pool.wait_ge(w_hi, n + 1)
                pool.tensor_tensor(dst[1][:, at:at + cols], stage[:, n % NSTG, 0:cols], dst[0][:, at:at + cols], ALU.subtract).then_inc(w_lo, 1)

            def rotate_sum(name, item, count):
                buf = ROT_BUF[name]
                pool.wait_ge(misc_free, item)
                pool.tensor_tensor(rot_a[buf][:], rot_a[buf][:], rot_b[buf][:], ALU.add).then_inc(rot_add, 1)
                dst = kT[1][:] if name == "k" else qT[1][:, int(name[1]) * S:(int(name[1]) + 1) * S]
                hi = kT[0][:] if name == "k" else qT[0][:, int(name[1]) * S:(int(name[1]) + 1) * S]
                pool.wait_ge(rot_hi, count)
                pool.tensor_tensor(dst, rot_a[buf][:], hi, ALU.subtract).then_inc(rot_lo, 1)

            def divide(h, par):
                pool.wait_ge(inverted, h + 1)
                for qt in range(QT):
                    pr = probs[par][:, P_AT[qt]:P_AT[qt] + (qt + 1) * P]
                    ins = pool.tensor_tensor(pr, pr, rinv[:, par, qt:qt + 1].to_broadcast([P, (qt + 1) * P]), ALU.mult)
                ins.then_inc(normed, 1)

            for n, name in enumerate(ROT):
                rotate_sum(name, n + 1, n + 1)
            divide(0, 0)

            def round_(i, last):
                base = PROJ_ITEMS + MISC_ROUND * i
                for j in range(GH - 1):
                    divide(i * GH + j + 1, (j + 1) % 2)
                    if not last:
                        rotate_sum(f"q{j}", base + j + 1, (i + 1) * 5 + j + 1)
                if not last:
                    rotate_sum("k", base + 4, (i + 1) * 5 + 4)
                    rotate_sum("q3", base + 5, (i + 1) * 5 + 5)
                    divide(i * GH + GH, 0)

            with pool.Fori(0, NG - 1) as i:
                round_(i, False)
            round_(NG - 1, True)

            def split_expert(e, par, loads, used):
                pool.wait_ge(exp_w_in[par], loads)
                if used is not None:
                    pool.wait_ge(down_ps, used)
                g = stage[:, par, 0:WG]
                d = stage[0:HC, par, WG:WG + WD]
                gs = [w[:, par * WG:(par + 1) * WG] for w in wg_s]
                dn = [w[0:HC, par * WD:(par + 1) * WD] for w in wd_s]
                pool.tensor_tensor(gs[0], g, one[:].to_broadcast([P, WG]), ALU.mult).then_inc(wg_hi, 1)
                pool.tensor_tensor(dn[0], d, one[0:HC, :].to_broadcast([HC, WD]), ALU.mult).then_inc(wd_hi, 1)
                pool.wait_ge(wg_hi, e + 1)
                pool.tensor_tensor(gs[1], g, gs[0], ALU.subtract)
                pool.wait_ge(wd_hi, e + 1)
                pool.tensor_tensor(dn[1], d, dn[0], ALU.subtract).then_inc(exp_w, 1)

            pool.wait_ge(zeroed, 4)
            for e in range(2):
                split_expert(e, e, 32, None)
            with pool.Fori(1, E_ROUTED // 2) as r:
                for par in range(2):
                    split_expert(r * 2 + par, par, r * 32 + 32, (r * 2 + par - 1) * NT)
            for half in range(2):
                split_expert(E_ROUTED + half, half, 32 * (E_ROUTED // 2) + 48, (E_ROUTED + half - 1) * NT)

        @block.scalar
        def _(act):
            act.dma_start(logit[:, 0:KC, :], gate_t.rearrange("(c p) e -> p c e", p=P)).then_inc(gate_in, 16)
            act.wait_ge(const_in, 64)
            act.copy(ident_b[:], ident_f[:]).then_inc(const_cast, 1)
            act.copy(mask_b[:], mask_f[:]).then_inc(const_cast, 1)
            act.wait_ge(gate_in, 16)
            act.copy(gate_s[0][:], logit[:, 0:KC, :].rearrange("p c e -> p (c e)")).then_inc(const_cast, 1)
            act.wait_ge(var_ready, 1)
            act.activation(root[:], var[:], ACT.Sqrt).then_inc(rooted, 1)
            for n, (dst, at, cols) in enumerate(W_CHUNKS):
                act.wait_ge(stage_in[n], 32 if n == 0 else 16)
                act.copy(dst[0][:, at:at + cols], stage[:, n % NSTG, 0:cols]).then_inc(w_hi, 1)
                if n < B:
                    for c in range(KC):
                        act.wait_ge(xnT_ps, n * KC + c + 1)
                        act.copy(xnT[0][:, c * TOK + n * S:c * TOK + (n + 1) * S], xnT_bank[c][:]).then_inc(xnT_hi, 1)
            act.wait_ge(rt, 2)
            act.activation(prob[:], prob[:], ACT.Exp).then_inc(rt_exp, 1)

            def rotate_hi(name, count):
                act.wait_ge(rot_add, count)
                dst = kT[0][:] if name == "k" else qT[0][:, int(name[1]) * S:(int(name[1]) + 1) * S]
                act.copy(dst, rot_a[ROT_BUF[name]][:]).then_inc(rot_hi, 1)

            def value_hi(item):
                act.wait_ge(misc_ps, item)
                act.copy(v_s[0][:], misc_bank[item_bank(6)][:]).then_inc(v_hi, 1)

            def exponentials(h, par):
                for u, unit in enumerate(SCORE_UNITS):
                    act.wait_ge(maxed, h * 3 + u + 1)
                    for qt, col in unit:
                        n = (qt + 1) * P
                        ins = act.activation(probs[par][:, P_AT[qt]:P_AT[qt] + n], score_bank[u][:, col:col + n], ACT.Exp,
                                             bias=nmax[:, par, qt:qt + 1], accum_out=rsum[:, par, qt:qt + 1])
                    ins.then_inc(exped, 1)

            def probs_hi(h, j):
                for u, (at, cols) in enumerate(PT_UNIT_COLS):
                    act.wait_ge(pt_ps, h * 3 + u + 1)
                    act.copy(pT[j % 2][0][:, at:at + cols], pt_bank[(3 * j + u) % 2][:, 0:cols]).then_inc(pt_hi, 1)

            def output_hi(h, j):
                act.wait_ge(pv, h + 1)
                act.copy(oT[0][:, j * S:(j + 1) * S], o_bank[:]).then_inc(o_hi, 1)

            for n, name in enumerate(ROT):
                rotate_hi(name, n + 1)
            value_hi(PROJ_ITEMS)
            exponentials(0, 0)

            def round_(i, last):
                base = PROJ_ITEMS + MISC_ROUND * i
                for j in range(GH - 1):
                    exponentials(i * GH + j + 1, (j + 1) % 2)
                    probs_hi(i * GH + j, j)
                    if j > 0:
                        output_hi(i * GH + j - 1, j - 1)
                    if not last:
                        rotate_hi(f"q{j}", (i + 1) * 5 + j + 1)
                probs_hi(i * GH + 3, 3)
                if not last:
                    rotate_hi("k", (i + 1) * 5 + 4)
                output_hi(i * GH + 2, 2)
                if not last:
                    rotate_hi("q3", (i + 1) * 5 + 5)
                    exponentials(i * GH + GH, 0)
                output_hi(i * GH + 3, 3)
                if not last:
                    value_hi(base + 6)

            with act.Fori(0, NG - 1) as i:
                round_(i, False)
            round_(NG - 1, True)

            def step(n, k, first, do_gu, do_t):
                if do_gu:
                    act.wait_ge(gu_ps, n + 1)
                    act.activation(sg[:, k % 2, :], gu_bank[k % 2][:, 0:INTER], ACT.Silu).then_inc(silued, 1)
                if do_t:
                    act.wait_ge(hT_ps, n)
                    act.copy(hT[0][:, (k - 1) % 4, :], hT_bank[(k - 1) % 2][0:HC, 0:2 * P]).then_inc(hT_hi, 1)

            for n in range(8):
                step(n, n, True, True, n >= 1)
            with act.Fori(2, STEPS // 4) as r:
                for k in range(4):
                    step(r * 4 + k, k, False, True, True)
            step(STEPS, 0, False, False, True)
            for b in range(B):
                act.wait_ge(y_done, STEPS)
                cols = slice(b * QT * D, (b + 1) * QT * D)
                act.activation(y_sb[:, cols], y_sb[:, cols], ACT.Silu).then_inc(gate_act, 1)

        @block.vector
        def _(dve):
            dve.wait_ge(const_cast, 3)
            dve.tensor_tensor(gate_s[1][:], logit[:, 0:KC, :].rearrange("p c e -> p (c e)"), gate_s[0][:], ALU.subtract).then_inc(ln_step, 1)
            dve.wait_ge(x_in, 16)
            for t in range(NT):
                dve.bn_stats(stats[:, t, :], x_sb[:, t * D:(t + 1) * D]).then_inc(ln_step, 1)
            dve.wait_ge(ln_step, NT + 1)
            for t in range(NT):
                dve.bn_aggr(mv[:, t, :], stats[:, t, :]).then_inc(ln_step, 1)
            dve.wait_ge(ln_step, 2 * NT + 1)
            dve.tensor_scalar(var[:], mv[:, :, 1], EPS, None, ALU.add).then_inc(var_ready, 1)
            dve.wait_ge(rooted, 1)
            dve.reciprocal(rstd[:], root[:]).then_inc(newton, 1)
            dve.wait_ge(newton, 1)
            dve.tensor_tensor(root[:], rstd[:], rstd[:], ALU.mult).then_inc(newton, 1)
            dve.wait_ge(newton, 2)
            dve.tensor_tensor(root[:], root[:], var[:], ALU.mult).then_inc(newton, 1)
            dve.wait_ge(newton, 3)
            dve.tensor_scalar(root[:], root[:], -0.5, 1.5, ALU.mult, ALU.add).then_inc(newton, 1)
            dve.wait_ge(newton, 4)
            dve.tensor_tensor(rstd[:], rstd[:], root[:], ALU.mult).then_inc(newton, 1)
            dve.wait_ge(newton, 5)
            for b in range(B):
                if b >= 1:
                    dve.wait_ge(xnT_ps, b * KC)
                for q in range(QT):
                    t = b * QT + q
                    ins = dve.tensor_scalar(xn[:, q * D:(q + 1) * D], x_sb[:, t * D:(t + 1) * D], mv[:, t, 0:1], rstd[:, t:t + 1],
                                            ALU.subtract, ALU.mult)
                ins.then_inc(xn_ready, 1)
                for c in range(KC):
                    at = c * TOK + b * S
                    dve.wait_ge(xnT_hi, b * KC + c + 1)
                    dve.tensor_tensor(xnT[1][:, at:at + S], xnT_bank[c][:], xnT[0][:, at:at + S], ALU.subtract).then_inc(xnT_lo, 1)
            dve.wait_ge(logit_ps, 1)
            dve.tensor_copy(logit[:], logit_bank[:, 0:NT * E_ROUTED].rearrange("p (t e) -> p t e", e=E_ROUTED)).then_inc(ln_step, 1)
            dve.wait_ge(ln_step, 2 * NT + 2)
            for t in range(NT):
                dve.max(top[:, t, :], logit[:, t, :]).then_inc(ln_step, 1)
            dve.wait_ge(ln_step, 3 * NT + 2)
            for t in range(NT):
                ins = dve.max_index(topi[:, t, :], top[:, t, :], logit[:, t, :])
            ins.then_inc(rt, 1)
            dve.tensor_tensor(prob[:], logit[:], top[:, :, 0:1].to_broadcast([P, NT, E_ROUTED]), ALU.subtract).then_inc(rt, 1)
            dve.wait_ge(rt, 2)
            dve.tensor_copy(topf[:], topi[:, :, 0:2]).then_inc(rt, 1)
            dve.wait_ge(rt, 3)
            e_of = iota_e[:].rearrange("p (o e) -> p o e", o=1).to_broadcast([P, NT, E_ROUTED])
            dve.tensor_tensor(sel[:], e_of, topf[:, :, 0:1].to_broadcast([P, NT, E_ROUTED]), ALU.is_equal).then_inc(rt, 1)
            dve.tensor_tensor(sel2[:], e_of, topf[:, :, 1:2].to_broadcast([P, NT, E_ROUTED]), ALU.is_equal).then_inc(rt, 1)
            dve.wait_ge(rt_exp, 1)
            dve.tensor_reduce(zsum[:], prob[:], AX.X, ALU.add).then_inc(rt, 1)
            dve.wait_ge(rt, 6)
            dve.tensor_tensor(sel[:], sel[:], sel2[:], ALU.add).then_inc(rt, 1)
            dve.reciprocal(zsum[:], zsum[:]).then_inc(rt, 1)
            dve.wait_ge(rt, 8)
            dve.tensor_tensor(sel[:], sel[:], prob[:], ALU.mult).then_inc(rt, 1)
            dve.wait_ge(rt, 9)
            dve.tensor_tensor(comb[:, 0:E_ROUTED * NT].rearrange("p (e t) -> p t e", t=NT), sel[:],
                              zsum[:].rearrange("p (t o) -> p t o", o=1).to_broadcast([P, NT, E_ROUTED]), ALU.mult).then_inc(rt, 1)

            def rotate_products(name, item, bank_n, freed):
                ps, buf = misc_bank[bank_n], ROT_BUF[name]
                cos, sin = (2, 3) if name == "k" else (0, 1)
                dve.wait_ge(misc_ps, item)
                if freed is not None:
                    dve.wait_ge(rot_lo, freed)
                dve.tensor_tensor(rot_a[buf][:], ps[:], tab[:, cos, :], ALU.mult)
                half = DH // 2
                dve.tensor_tensor(rot_b[buf][0:half, :], ps[half:DH, :], tab[half:DH, sin, :], ALU.mult)
                dve.tensor_tensor(rot_b[buf][half:DH, :], ps[0:half, :], tab[0:half, sin, :], ALU.mult).then_inc(misc_free, 1)

            def value_lo(round_n):
                dve.wait_ge(v_hi, round_n)
                dve.tensor_tensor(v_s[1][:], misc_bank[item_bank(6)][:], v_s[0][:], ALU.subtract).then_inc(misc_free, 1)

            def row_max(h, par):
                for u, unit in enumerate(SCORE_UNITS):
                    dve.wait_ge(scores, h * 3 + u + 1)
                    for qt, col in unit:
                        ins = dve.tensor_reduce(nmax[:, par, qt:qt + 1], score_bank[u][:, col:col + (qt + 1) * P], AX.X, ALU.max, negate=True)
                    ins.then_inc(maxed, 1)

            def invert_sums(h, par):
                dve.wait_ge(exped, h * 3 + 3)
                dve.reciprocal(rinv[:, par, :], rsum[:, par, :]).then_inc(inverted, 1)

            def probs_lo(h, j, units):
                for u in units:
                    at, cols = PT_UNIT_COLS[u]
                    dve.wait_ge(pt_hi, h * 3 + u + 1)
                    dve.tensor_tensor(pT[j % 2][1][:, at:at + cols], pt_bank[(3 * j + u) % 2][:, 0:cols], pT[j % 2][0][:, at:at + cols],
                                      ALU.subtract).then_inc(pt_lo, 1)

            def output_lo(h, j):
                dve.wait_ge(o_hi, h + 1)
                sl = slice(j * S, (j + 1) * S)
                dve.tensor_tensor(oT[1][:, sl], o_bank[:], oT[0][:, sl], ALU.subtract).then_inc(o_lo, 1)

            def add_projection(i, item, half):
                at = (i // NKV) * (QT * D) + half * 512
                dve.wait_ge(misc_ps, item)
                dve.wait_ge(misc_free, item - 1)
                dve.tensor_tensor(s_sb[:, bass.ds(at, 512)], misc_bank[item_bank(7 + half)][:], s_sb[:, bass.ds(at, 512)], ALU.add).then_inc(misc_free, 1)

            dve.wait_ge(const_in, 64)
            for n, name in enumerate(ROT):
                rotate_products(name, n + 1, item_bank(n + 1), {2: 1, 4: 2}.get(n))
            value_lo(1)
            row_max(0, 0)
            invert_sums(0, 0)
            dve.wait_ge(zeroed, 4)

            def round_(i, last):
                base = PROJ_ITEMS + MISC_ROUND * i
                freed = {"q0": i * 5 + 3, "q1": i * 5 + 5, "q2": i * 5 + 6, "k": i * 5 + 4, "q3": i * 5 + 7}
                for j in range(GH - 1):
                    row_max(i * GH + j + 1, (j + 1) % 2)
                    probs_lo(i * GH + j, j, (0, 1))
                    invert_sums(i * GH + j + 1, (j + 1) % 2)
                    if not last:
                        rotate_products(f"q{j}", base + j + 1, item_bank(j + 1), freed[f"q{j}"])
                    probs_lo(i * GH + j, j, (2,))
                    if j > 0:
                        output_lo(i * GH + j - 1, j - 1)
                probs_lo(i * GH + 3, 3, (0, 1))
                if not last:
                    rotate_products("k", base + 4, item_bank(4), freed["k"])
                probs_lo(i * GH + 3, 3, (2,))
                if not last:
                    rotate_products("q3", base + 5, item_bank(5), freed["q3"])
                output_lo(i * GH + 2, 2)
                if not last:
                    row_max(i * GH + GH, 0)
                output_lo(i * GH + 3, 3)
                if not last:
                    invert_sums(i * GH + GH, 0)
                    value_lo(i + 2)
                ops = base + (0 if last else PROJ_ITEMS)
                for half in range(2):
                    add_projection(i, ops + half + 1, half)

            with dve.Fori(0, NG - 1) as i:
                round_(i, False)
            round_(NG - 1, True)

            def step(n, k, first, do_gu, do_t, do_y):
                if do_gu:
                    dve.wait_ge(silued, n + 1)
                    dve.tensor_tensor(hid[:, k % 2, :], gu_bank[k % 2][:, INTER:GU], sg[:, k % 2, :], ALU.mult).then_inc(hidden, 1)
                if do_t:
                    dve.wait_ge(hT_hi, n)
                    dve.tensor_tensor(hT[1][:, (k - 1) % 4, :], hT_bank[(k - 1) % 2][0:HC, 0:2 * P], hT[0][:, (k - 1) % 4, :],
                                      ALU.subtract).then_inc(hT_lo, 1)
                if do_y:
                    m = n - 3
                    yt = y_sb[:, bass.ds((m % NT) * D, D)]
                    dve.wait_ge(down_ps, m + 1)
                    if not (first and n == 3):
                        dve.wait_ge(y_done, m)
                    dve.scalar_tensor_tensor(out=yt, in0=y_bank[(k - 3) % 2][:, 0:D], scalar=comb[:, bass.ds(m, 1)], in1=yt,
                                             op0=ALU.mult, op1=ALU.add).then_inc(y_done, 1)

            dve.wait_ge(rt, 10)
            for n in range(8):
                step(n, n, True, True, n >= 1, n >= 3)
            with dve.Fori(2, STEPS // 4) as r:
                for k in range(4):
                    step(r * 4 + k, k, False, True, True, True)
            for n in range(STEPS, STEPS + 3):
                step(n, n % 4, False, False, n == STEPS, True)
            for b in range(B):
                cols = slice(b * QT * D, (b + 1) * QT * D)
                dve.wait_ge(gate_act, b + 1)
                dve.tensor_tensor(s_sb[:, cols], s_sb[:, cols], y_sb[:, cols], ALU.mult).then_inc(gated, 1)
                dve.wait_ge(gated, b + 1)
                dve.tensor_tensor(s_sb[:, cols], s_sb[:, cols], x_sb[:, cols], ALU.add).then_inc(summed, 1)

        @block.tensor
        def _(pe):
            pe.wait_ge(const_in, 64)
            for b in range(B):
                pe.wait_ge(xn_ready, b + 1)
                for c in range(KC):
                    if b >= 1:
                        pe.wait_ge(xnT_lo, (b - 1) * KC + c + 1)
                    for q in range(QT):
                        ins = pe.transpose(xnT_bank[c][:, q * P:(q + 1) * P], xn[:, q * D + c * P:q * D + (c + 1) * P], ident_f[:])
                    ins.then_inc(xnT_ps, 1)
            pe.wait_ge(xnT_lo, B * KC)
            pe.wait_ge(ln_step, 1)
            for t in range(NT):
                for c in range(KC):
                    for n, (a, m) in enumerate(PASSES):
                        ins = pe.matmul(logit_bank[:, t * E_ROUTED:(t + 1) * E_ROUTED], xnT[a][:, c * TOK + t * P:c * TOK + (t + 1) * P],
                                        gate_s[m][:, c * E_ROUTED:(c + 1) * E_ROUTED],
                                        start=(c == 0 and n == 0), stop=(c == KC - 1 and n == 2))
            ins.then_inc(logit_ps, 1)

            def project(name, i, bank_n, item):
                b, g = i // NKV, i % NKV
                if item is not None:
                    pe.wait_ge(misc_free, item - 2)
                for c in range(KC):
                    for n, (a, m) in enumerate(PASSES):
                        if name == "k":
                            w = wkv_s[a][:, bass.ds(c * 512 + g * DH, DH)]
                        else:
                            w = wq_s[a][:, bass.ds(c * 2048 + g * (GH * DH) + int(name[1]) * DH, DH)]
                        ins = pe.matmul(misc_bank[bank_n][:], w, xnT[m][:, bass.ds(c * TOK + b * S, S)],
                                        start=(c == 0 and n == 0), stop=(c == KC - 1 and n == 2))
                ins.then_inc(misc_ps, 1)

            def project_values(i, item):
                b, g = i // NKV, i % NKV
                pe.wait_ge(misc_free, item - 2)
                for q in range(QT):
                    for c in range(KC):
                        for n, (a, m) in enumerate(PASSES):
                            ins = pe.matmul(misc_bank[item_bank(6)][:, q * DH:(q + 1) * DH],
                                            xnT[a][:, bass.ds(c * TOK + b * S + q * P, P)],
                                            wkv_s[m][:, bass.ds(1024 + c * 512 + g * DH, DH)],
                                            start=(c == 0 and n == 0), stop=(c == KC - 1 and n == 2))
                ins.then_inc(misc_ps, 1)

            def score(h, j, queries, keys, reuse):
                pe.wait_ge(rot_lo, queries)
                if keys is not None:
                    pe.wait_ge(rot_lo, keys)
                for u, unit in enumerate(SCORE_UNITS):
                    if reuse:
                        pe.wait_ge(exped, h * 3 + u - 2)
                    for qt, col in unit:
                        n_k = (qt + 1) * P
                        for n, (a, m) in enumerate(PASSES):
                            pe.matmul(score_bank[u][:, col:col + n_k], qT[a][:, j * S + qt * P:j * S + (qt + 1) * P], kT[m][:, 0:n_k],
                                      start=(n == 0), stop=False)
                        ins = pe.matmul(score_bank[u][:, col + qt * P:col + n_k], ident_b[:], mask_b[:], start=False, stop=True)
                    ins.then_inc(scores, 1)

            def transpose_probs(h, j, units):
                for u in units:
                    if u == 0:
                        pe.wait_ge(normed, h + 1)
                    if not (j == 0 and u < 2):
                        pe.wait_ge(pt_lo, h * 3 + u - 1)
                    for kt, col in PT_UNITS[u]:
                        for qt in range(kt, QT):
                            ins = pe.transpose(pt_bank[(3 * j + u) % 2][:, col + (qt - kt) * P:col + (qt - kt + 1) * P],
                                               probs[j % 2][:, P_AT[qt] + kt * P:P_AT[qt] + (kt + 1) * P], ident_f[:])
                    ins.then_inc(pt_ps, 1)

            def weigh_values(h, j, i):
                pe.wait_ge(pt_lo, h * 3 + 3)
                if j == 0:
                    pe.wait_ge(misc_free, PROJ_ITEMS + MISC_ROUND * i)
                else:
                    pe.wait_ge(o_lo, h)
                for kt in range(QT):
                    n_q = (QT - kt) * P
                    for n, (a, m) in enumerate(PASSES):
                        ins = pe.matmul(o_bank[:, kt * P:S], v_s[a][:, kt * DH:(kt + 1) * DH], pT[j % 2][m][:, PT_AT[kt]:PT_AT[kt] + n_q],
                                        start=(kt == 0 and n == 0), stop=(kt == QT - 1 and n == 2))
                ins.then_inc(pv, 1)

            def project_out(i, half, item):
                g = i % NKV
                pe.wait_ge(o_lo, i * GH + GH)
                pe.wait_ge(misc_free, item - 2)
                for q in range(2):
                    tok = (half * 2 + q) * P
                    for j in range(GH):
                        for n, (a, m) in enumerate(PASSES):
                            ins = pe.matmul(misc_bank[item_bank(7 + half)][:, q * D:(q + 1) * D], oT[a][:, j * S + tok:j * S + tok + P],
                                            wo_s[m][:, bass.ds(g * (GH * D) + j * D, D)],
                                            start=(j == 0 and n == 0), stop=(j == GH - 1 and n == 2))
                ins.then_inc(misc_ps, 1)

            pe.wait_ge(w_lo, N_CHUNKS)
            pe.wait_ge(const_cast, 2)
            for n, name in enumerate(ROT):
                project(name, 0, item_bank(n + 1), n + 1 if n >= 2 else None)
            project_values(0, PROJ_ITEMS)
            pe.wait_ge(rt, 1)
            score(0, 0, 1, 4, False)

            def round_(i, last):
                base = PROJ_ITEMS + MISC_ROUND * i
                q_ready = [i * 5 + 1, i * 5 + 2, i * 5 + 3, i * 5 + 5]
                for j in range(GH):
                    if j < GH - 1:
                        score(i * GH + j + 1, j + 1, q_ready[j + 1], None, True)
                    transpose_probs(i * GH + j, j, (0, 1))
                    if not last:
                        name = f"q{j}" if j < 3 else "k"
                        project(name, i + 1, item_bank(j + 1), base + j + 1)
                    transpose_probs(i * GH + j, j, (2,))
                    if j == 3 and not last:
                        project("q3", i + 1, item_bank(5), base + 5)
                    if j >= 1:
                        weigh_values(i * GH + j - 1, j - 1, i)
                if not last:
                    score(i * GH + GH, 0, (i + 1) * 5 + 1, (i + 1) * 5 + 4, True)
                weigh_values(i * GH + 3, 3, i)
                if not last:
                    project_values(i + 1, base + 6)
                ops = base + (0 if last else PROJ_ITEMS)
                for half in range(2):
                    project_out(i, half, ops + half + 1)

            with pe.Fori(0, NG - 1) as i:
                round_(i, False)
            round_(NG - 1, True)

            def step(n, k, first, do_gu, do_t, do_y):
                if do_gu:
                    t, e = n % NT, n // NT
                    pe.wait_ge(exp_w, e + 1)
                    if not (first and n < 2):
                        pe.wait_ge(hidden, n - 1)
                    for c in range(KC):
                        for p, (a, m) in enumerate(PASSES):
                            ins = pe.matmul(gu_bank[k % 2][:, 0:GU], xnT[a][:, bass.ds(c * TOK + t * P, P)],
                                            wg_s[m][:, bass.ds((e % 2) * WG + c * GU, GU)],
                                            start=(c == 0 and p == 0), stop=(c == KC - 1 and p == 2))
                    ins.then_inc(gu_ps, 1)
                if do_y:
                    d = n - 3
                    pe.wait_ge(hT_lo, d + 1)
                    if not (first and n < 5):
                        pe.wait_ge(y_done, d - 1)
                    for c in range(2):
                        for p, (a, m) in enumerate(PASSES):
                            ins = pe.matmul(y_bank[(k - 3) % 2][:, 0:D], hT[a][:, (k - 3) % 4, c * P:(c + 1) * P],
                                            wd_s[m][0:HC, bass.ds(((d // NT) % 2) * WD + c * D, D)],
                                            start=(c == 0 and p == 0), stop=(c == 1 and p == 2))
                    ins.then_inc(down_ps, 1)
                if do_t:
                    pe.wait_ge(hidden, n)
                    if not (first and n < 3):
                        pe.wait_ge(hT_lo, n - 2)
                    for c in range(2):
                        ins = pe.transpose(hT_bank[(k - 1) % 2][0:HC, c * P:(c + 1) * P], hid[:, (k - 1) % 2, c * HC:(c + 1) * HC], ident_f[:])
                    ins.then_inc(hT_ps, 1)

            pe.wait_ge(misc_free, PROJ_ITEMS + MISC_ROUND * (NG - 1) + 2)
            for n in range(8):
                step(n, n, True, True, n >= 1, n >= 3)
            with pe.Fori(2, STEPS // 4) as r:
                for k in range(4):
                    step(r * 4 + k, k, False, True, True, True)
            for n in range(STEPS, STEPS + 3):
                step(n, n % 4, False, False, n == STEPS, True)


def item_bank(n):
    return (n - 1) % 2


def kernel(**inputs):
    import numpy as np
    import concourse.bacc as bacc
    from concourse.bass_utils import run_bass_kernel_spmd

    pos = np.arange(S, dtype=np.float32)
    half = DH // 2
    inv_freq = (1.0 / 10000.0 ** (np.arange(half, dtype=np.float32) / np.float32(half))).astype(np.float32)
    freqs = np.outer(pos, inv_freq).astype(np.float32)
    cos = np.cos(np.concatenate([freqs, freqs], -1)).astype(np.float64)
    sin = np.sin(np.concatenate([freqs, freqs], -1)).astype(np.float64)
    scale = (pos.astype(np.float64) + 32.0) / 64.0
    xs = np.stack([np.repeat(scale[:, None], half, 1), np.repeat(1.0 / scale[:, None], half, 1)], -1).reshape(S, DH)
    sgn = np.concatenate([-np.ones(half), np.ones(half)])
    qs, ks = xs / np.sqrt(DH), 1.0 / xs
    tables = [cos * qs, np.roll(sin * sgn * qs, -half, 1), cos * ks, np.roll(sin * sgn * ks, -half, 1)]
    rope = np.ascontiguousarray(np.stack([t.T for t in tables]).astype(np.float32))

    arrays = {
        "x": inputs["L0_attn_x"], "wq": inputs["L0_attn_Wq"], "wk": inputs["L0_attn_Wk"], "wv": inputs["L0_attn_Wv"],
        "wo": inputs["L0_attn_Wo"], "gate_t": np.asarray(inputs["L0_ffn_gate_w"]).T, "w_gate_up": inputs["L0_ffn_w_gate_up"],
        "w_down": inputs["L0_ffn_w_down"], "shared_gu": inputs["L0_ffn_shared_gate_up"], "shared_down": inputs["L0_ffn_shared_down"],
        "rope": rope, "ident": np.eye(P, dtype=np.float32),
        "mask": np.where(np.tril(np.ones((P, P), bool)), 0.0, -1e30).astype(np.float32),
        "eidx": np.tile(np.arange(E_ROUTED, dtype=np.float32), (P, 1)),
    }
    arrays = {n: np.ascontiguousarray(a) for n, a in arrays.items()}
    nc = bacc.Bacc("TRN2", target_bir_lowering=False, num_devices=1)
    aps = [nc.dram_tensor(n, a.shape, mybir.dt.from_np(a.dtype), kind="ExternalInput").ap() for n, a in arrays.items()]
    aps.append(nc.dram_tensor("out", (B, S, D), F32, kind="ExternalOutput").ap())
    build(nc, *aps)
    return run_bass_kernel_spmd(nc, [arrays], core_ids=[0]).results[0]["out"]
```

```python
from contextlib import ExitStack

import concourse.bass as bass
from concourse import mybir

F32 = mybir.dt.float32
F16 = mybir.dt.float16
BF16 = mybir.dt.bfloat16
U32 = mybir.dt.uint32
ACT = mybir.ActivationFunctionType
ALU = mybir.AluOpType
AX = mybir.AxisListType

P = 128
B, S, D = 4, 512, 256
KC = D // P
TOK = B * S
NT = TOK // P
QT = S // P
NH, NKV, DH = 16, 4, 128
GH = NH // NKV
NG = B * NKV
E_ROUTED, INTER, TOP_K = 16, 176, 2
E_SHARED = 2
HC = INTER // 2
GU = 2 * INTER
WG, WD = KC * GU, 2 * D
WE = WG + WD
R_TILES = (TOP_K * TOK + E_ROUTED * (P - 1)) // P
R_TILES = -(-R_TILES // 4) * 4
DX = D + 2
SH_STEPS = E_SHARED * NT
SH_FIRST = 16
ROUTED_END = SH_FIRST + R_TILES
STEPS = SH_STEPS + R_TILES
LAG = 3
EPS = 1e-5

SCORE_UNITS = [[(3, 0)], [(2, 0), (0, 384)], [(1, 0)]]
PT_UNITS = [[(0, 0)], [(1, 0), (3, 384)], [(2, 0)]]
PT_AT = {0: 0, 1: 512, 3: 896, 2: 1024}
PT_UNIT_COLS = [(0, 512), (512, 512), (1024, 256)]
P_AT = [0, 128, 384, 768]
PCOLS = 1280

ITEMS_FIRST = ["q0", "q1", "q2", "k", "q3", "v"]
ITEMS_LOOP = ["q0", "o0", "q1", "o1", "q2", "o2", "k", "q3", "o3", "v"]
ITEMS_LAST = ["o0", "o1", "o2", "o3"]
ROT = ["q0", "q1", "q2", "k", "q3"]
ROT_BUF = {"q0": 0, "q1": 1, "q2": 0, "k": 2, "q3": 1}


class Round:

    def __init__(self, i, kind):
        self.i, self.first, self.last = i, kind == "first", kind == "last"
        self.items = {"first": ITEMS_FIRST, "loop": ITEMS_LOOP, "last": ITEMS_LAST}[kind]
        self.base = len(ITEMS_FIRST) if self.first else len(ITEMS_LOOP) * i + 2 * len(ITEMS_FIRST) - len(ITEMS_LOOP)

    def item(self, name):
        return self.base + self.items.index(name) + 1

    def bank(self, name):
        return self.items.index(name) % 2

    def head(self, j):
        return self.i * GH + j

    def rot(self, name):
        return (self.i + 1) * len(ROT) + ROT.index(name) + 1


PROLOGUE = Round(-1, "first")
PROLOGUE.base = 0
EPILOGUE = Round(NG, "last")
EPILOGUE.base = Round(NG - 1, "last").base + len(ITEMS_LAST)
ATTENTION_ITEMS = EPILOGUE.base + len(ITEMS_LAST)


class Step:

    def __init__(self, n, like):
        self.n, self.like = n, like
        self.gu = like < STEPS
        self.t = 1 <= like <= STEPS
        self.y = like >= LAG
        self.rows = SH_FIRST <= like + 2 < ROUTED_END

    def routed(self, back=0):
        return SH_FIRST <= self.like - back < ROUTED_END

    def tile(self, back=0):
        if self.routed(back):
            return self.n - (back + SH_FIRST)
        return self.n - back if self.like - back < SH_FIRST else self.n - (back + R_TILES)

    def ring(self, of, back=0):
        return (self.like - back) % of


def ffn_steps(engine, step):
    at = 0
    for lo, hi in ((SH_FIRST + 8, ROUTED_END - 4), (ROUTED_END + 8, STEPS)):
        for n in range(at, lo):
            step(Step(n, n))
        with engine.Fori(lo // 4, hi // 4) as r:
            for k in range(4):
                step(Step(r * 4 + k, lo + k))
        at = hi
    for n in range(STEPS, STEPS + LAG):
        step(Step(n, n))


def build(nc, x, wq, wk, wv, wo, gate_t, w_gate_up, w_down, shared_gu, shared_down, rope, ident, mask, iota, tri, rows, out):
    with ExitStack() as ctx:
        def sb(name, shape, dt):
            return ctx.enter_context(nc.sbuf_tensor(name, shape, dt))

        def sem(name):
            return ctx.enter_context(nc.semaphore(name))

        ident_f = sb("ident_f", [P, P], F32)
        ident_b = sb("ident_b", [P, P], BF16)
        mask_b = sb("mask_b", [P, P], BF16)
        tri_b = sb("tri_b", [P, P], BF16)
        ones_b = sb("ones_b", [P, P], BF16)
        one = sb("one", [P, 1], F32)
        iota_f = sb("iota_f", [P, R_TILES], F32)
        tab = sb("tab", [P, 4, S], F32)
        s_sb = sb("s_sb", [P, NT * D], F32)
        row_id = sb("row_id", [P, TOP_K * NT + R_TILES], F32)
        xn = sb("xn", [P, NT * DX], F32)
        xn_t = xn[:].rearrange("p (t d) -> p t d", d=DX)
        y_sb = xn[:, 0:NT * D]
        xnT = [sb("xnT_hi", [P, KC * TOK], F16), sb("xnT_lo", [P, KC * TOK], BF16)]
        stats = sb("stats", [P, NT, 6], F32)
        mv = sb("mv", [P, NT, 2], F32)
        rstd = sb("rstd", [P, NT], F32)
        var = sb("var", [P, NT], F32)
        root = sb("root", [P, NT], F32)
        gate_f = sb("gate_f", [P, KC, E_ROUTED], F32)
        gate_s = [sb("gate_hi", [P, KC * E_ROUTED], F16), sb("gate_lo", [P, KC * E_ROUTED], BF16)]
        logit = sb("logit", [P, NT, E_ROUTED], F32)
        top = sb("top", [P, NT, 8], F32)
        topi = sb("topi", [P, NT, 8], U32)
        topf = sb("topf", [P, NT, 2], F32)
        sel = [sb(f"sel{n}", [P, NT, E_ROUTED], F32) for n in range(TOP_K)]
        sel_b = sb("sel_b", [P, NT * E_ROUTED], BF16)
        prob = sb("prob", [P, NT, E_ROUTED], F32)
        pick = [sb(f"pick{n}", [P, NT, E_ROUTED], F32) for n in range(TOP_K)]
        zsum = sb("zsum", [P, NT], F32)
        weight = sb("weight", [P, TOP_K, NT], F32)
        count = sb("count", [P, E_ROUTED, NT], F32)
        total = sb("total", [P, E_ROUTED, NT], F32)
        ends = sb("ends", [P, E_ROUTED + 1], F32)
        held = sb("held", [P, E_ROUTED], F32)
        steps128 = sb("steps128", [P, E_ROUTED], F32)
        compare = sb("compare", [P, R_TILES * E_ROUTED], F32)
        mask_f, tri_f = compare[:, 0:P], compare[:, P:2 * P]
        tiles = sb("tiles", [P, E_ROUTED], F32)
        tiles_to = sb("tiles_to", [P, E_ROUTED], F32)
        offset = sb("offset", [P, E_ROUTED], F32)
        slot = logit
        slot_f = sb("slot_f", [P, TOP_K, NT], F32)
        slot_u = sb("slot_u", [P, TOP_K, NT], U32)
        tile_e = sb("tile_e", [1, R_TILES], F32)
        tile_u = sb("tile_u", [1, R_TILES], U32)
        meta = sb("meta", [P, R_TILES, 2], F32)
        NSTG, SCOLS = 3, 2048
        stage = sb("stage", [P, NSTG * SCOLS], F32)
        ERING = 5
        shared_s = [sb("shared_hi", [P, E_SHARED * WE], F16), sb("shared_lo", [P, E_SHARED * WE], BF16)]

        ARENA = 102400
        arena = sb("arena", [P, ARENA // 4], F32)
        taken = [0]

        def carve(cols, dt):
            size = 4 if dt == F32 else 2
            a = taken[0]
            taken[0] = a + cols * size // 4
            assert taken[0] * 4 <= ARENA
            return arena[:, a:taken[0]] if dt == F32 else arena[:, a:taken[0]].bitcast(dt)

        def split(cols):
            return [carve(cols, F16), carve(cols, BF16)]

        wkv_s, wq_s, wo_s = split(2 * KC * 512), split(KC * 2048), split(NH * D)
        qT, kT, v_s = split(GH * S), split(S), split(S)
        rot_a = [carve(S, F32) for _ in range(3)]
        rot_b = [carve(S, F32) for _ in range(3)]
        probs = [carve(PCOLS, F32) for _ in range(2)]
        pT = [split(PCOLS) for _ in range(2)]
        x_sb = arena[:, taken[0]:taken[0] + NT * D]
        oT = split(2 * GH * S)
        taken[0] = 0
        xT = [split(KC * P) for _ in range(2)]
        xs = carve(4 * D, F32).rearrange("p (r d) -> p r d", r=4)
        ys = carve(4 * D, F32).rearrange("p (r d) -> p r d", r=4)
        sg = carve(2 * INTER, F32).rearrange("p (r n) -> p r n", r=2)
        hid = carve(2 * INTER, F32).rearrange("p (r n) -> p r n", r=2)
        hT = [w[0:HC, :].rearrange("p (r n) -> p r n", r=4) for w in split(4 * 2 * P)]
        expert_s = split(E_ROUTED * WE)
        nmax = sb("nmax", [P, 2, QT], F32)
        rsum = sb("rsum", [P, 2, QT], F32)
        rinv = sb("rinv", [P, 2, QT], F32)
        BACK = 2
        BRING = 4
        back_cols = BRING * BACK * TOP_K * D
        back = stage[:, 0:back_cols].rearrange("p (r t k d) -> p r t k d", r=BRING, t=BACK, k=TOP_K)
        x_back = stage[:, back_cols:back_cols + BRING * BACK * D].rearrange("p (r t d) -> p r t d", r=BRING, t=BACK)

        xs_dram = nc.dram_tensor("xs_dram", (R_TILES * P, DX), F32).ap()
        ys_dram = nc.dram_tensor("ys_dram", ((TOP_K * NT + R_TILES) * P, D), F32).ap()

        bank = [ctx.enter_context(nc.psum_tensor(f"bank{n}", [P, 512], F32)) for n in range(8)]
        score_bank, pt_bank, o_bank, misc_bank = bank[0:3], bank[3:5], bank[5], bank[6:8]
        gu_bank, hT_bank, y_bank, xT_bank = bank[0:2], bank[2:4], bank[4:6], bank[6:8]
        xnT_bank, logit_bank, rank_bank = bank[6:8], bank[5], bank[5]

        x_in, const_in, gate_in = sem("x_in"), sem("const_in"), sem("gate_in")
        stage_in = [sem(f"stage_in{n}") for n in range(5)]
        const_cast, zeroed, filled, xs_filled = sem("const_cast"), sem("zeroed"), sem("filled"), sem("xs_filled")
        w_hi, w_lo = sem("w_hi"), sem("w_lo")
        var_ready, rooted, newton = sem("var_ready"), sem("rooted"), sem("newton")
        ln_step, xn_ready, xnT_ps, xnT_hi, xnT_lo = sem("ln_step"), sem("xn_ready"), sem("xnT_ps"), sem("xnT_hi"), sem("xnT_lo")
        logit_ps, rt, rt_shift, rt_exp = sem("logit_ps"), sem("rt"), sem("rt_shift"), sem("rt_exp")
        chosen, rank_ps, ranks_read, slots_ready = sem("chosen"), sem("rank_ps"), sem("ranks_read"), sem("slots_ready")
        first_meta, second_meta, first_scattered, second_scattered = (
            sem("first_meta"), sem("second_meta"), sem("first_scattered"), sem("second_scattered"))
        meta_in = sem("meta_in")
        scores, maxed, exped, inverted, normed = sem("scores"), sem("maxed"), sem("exped"), sem("inverted"), sem("normed")
        pt_ps, pt_hi, pt_lo = sem("pt_ps"), sem("pt_hi"), sem("pt_lo")
        pv, o_hi, o_lo = sem("pv"), sem("o_hi"), sem("o_lo")
        misc_ps, misc_free = sem("misc_ps"), sem("misc_free")
        rot_add, rot_hi, rot_lo, v_hi = sem("rot_add"), sem("rot_hi"), sem("rot_lo"), sem("v_hi")
        shared_in, shared_hi, shared_w = sem("shared_in"), sem("shared_hi"), sem("shared_w")
        expert_in = [sem(f"expert_in{n}") for n in range(ERING)]
        expert_hi, even_lo, odd_lo = sem("expert_hi"), sem("even_lo"), sem("odd_lo")
        xs_in = [sem(f"xs_in{n}") for n in range(4)]
        ys_out = [sem(f"ys_out{n}") for n in range(4)]
        xT_ps, xT_hi, xT_lo, ys_ready = sem("xT_ps"), sem("xT_hi"), sem("xT_lo"), sem("ys_ready")
        gu_ps, silued, hidden, hT_ps, hT_hi, hT_lo, down_ps, y_done = (
            sem("gu_ps"), sem("silued"), sem("hidden"), sem("hT_ps"), sem("hT_hi"), sem("hT_lo"), sem("down_ps"), sem("y_done"))
        back_in = [sem(f"back_in{n}") for n in range(BRING)]
        pair_sum, ffn_sum, gate_act, gated, summed, stored = sem("pair_sum"), sem("ffn_sum"), sem("gate_act"), sem("gated"), sem("summed"), sem("stored")

        PASSES = ((0, 0), (0, 1), (1, 0))

        W_CHUNKS = [(wkv_s, 0, 2048), (wq_s, 0, 2048), (wq_s, 2048, 2048), (wo_s, 0, 2048), (wo_s, 2048, 2048)]
        N_CHUNKS = len(W_CHUNKS)
        FILLS = 4
        FILL_TILES = R_TILES // FILLS
        fill = s_sb[:, 0:FILL_TILES * DX].rearrange("p (t d) -> p t d", d=DX)
        def expert_lo(engine, e):
            at, st = e * WE, e % ERING * WE
            for rows_, a, b in ((slice(0, P), 0, WG), (slice(0, HC), WG, WE)):
                ins = engine.tensor_tensor(expert_s[1][rows_, at + a:at + b], stage[rows_, st + a:st + b],
                                           expert_s[0][rows_, at + a:at + b], ALU.subtract)
            return ins

        block = ctx.enter_context(nc.Block())

        @block.sync
        def _(sp):
            sp.dma_start(x_sb.rearrange("p (t d) -> p t d", d=D), x.rearrange("b (t p) d -> p (b t) d", p=P)).then_inc(x_in, 16)
            sp.dma_start(ident_f[:], ident).then_inc(const_in, 16)
            sp.dma_start(mask_f, mask).then_inc(const_in, 16)
            sp.dma_start(tri_f, tri).then_inc(const_in, 16)
            sp.dma_start(iota_f[:], iota).then_inc(const_in, 16)
            sp.dma_start(row_id[:], rows).then_inc(const_in, 16)

            def stg(n):
                return stage[:, n * SCOLS:(n + 1) * SCOLS]

            sp.dma_start(stg(0)[:, 0:1024].rearrange("p (c n) -> p c n", c=KC), wk.rearrange("(c p) n -> p c n", p=P)).then_inc(stage_in[0], 16)
            sp.dma_start(stg(0)[:, 1024:2048].rearrange("p (c n) -> p c n", c=KC), wv.rearrange("(c p) n -> p c n", p=P)).then_inc(stage_in[0], 16)
            sp.dma_start(stg(1), wq[0:P, :]).then_inc(stage_in[1], 16)
            sp.dma_start(stg(2), wq[P:2 * P, :]).then_inc(stage_in[2], 16)
            sp.dma_start(tab[:], rope.rearrange("a p s -> p a s")).then_inc(const_in, 16)
            for half in range(2):
                sp.wait_ge(w_lo, half + 1)
                sp.dma_start(stg(half).rearrange("p (h n) -> p h n", n=D),
                             wo[half * 1024:(half + 1) * 1024, :].rearrange("(h p) n -> p h n", p=P)).then_inc(stage_in[3 + half], 16)
            sp.wait_ge(filled, 1)
            xs_tiles = xs_dram.rearrange("(t p) d -> p t d", p=P)
            for c in range(FILLS):
                sp.dma_start(xs_tiles[:, c * FILL_TILES:(c + 1) * FILL_TILES], fill).then_inc(xs_filled, 16)

            sp.wait_ge(w_lo, N_CHUNKS)
            for half in range(E_SHARED):
                at = half * WE
                for c in range(KC):
                    sp.dma_start(stage[:, at + c * GU:at + (c + 1) * GU].rearrange("p (w n) -> p w n", w=2),
                                 shared_gu[c * P:(c + 1) * P, :].rearrange("p (w n) -> p w n", w=2)[:, :, half * INTER:(half + 1) * INTER]
                                 ).then_inc(shared_in, 16)
                sp.dma_start(stage[0:HC, at + WG:at + WE].rearrange("p (c n) -> p c n", c=2),
                             shared_down[half * INTER:(half + 1) * INTER, :].rearrange("(c p) n -> p c n", p=HC)).then_inc(shared_in, 16)

            sp.wait_ge(shared_w, 1)
            for e in range(E_ROUTED):
                if e >= ERING:
                    sp.wait_ge(odd_lo if (e - ERING) % 2 else even_lo, (e - ERING) // 2 + 1)
                at = e % ERING * WE
                sp.dma_start(stage[:, at:at + WG].rearrange("p (c n) -> p c n", c=KC),
                             w_gate_up[e].rearrange("(c p) n -> p c n", p=P)).then_inc(expert_in[e % ERING], 16)
                sp.dma_start(stage[0:HC, at + WG:at + WE].rearrange("p (c n) -> p c n", c=2),
                             w_down[e].rearrange("(c p) n -> p c n", p=HC)).then_inc(expert_in[e % ERING], 16)
                if e == ERING - 1:
                    sp.wait_ge(first_scattered, 16 * NT)
                    sp.wait_ge(second_scattered, 16 * NT)
                    sp.dma_start(meta[:], xs_tiles[:, :, D:DX]).then_inc(meta_in, 16)

            def load_rows(m, k):
                sp.dma_start(xs[:, k, :], xs_dram[bass.ds(m * P, P), 0:D]).then_inc(xs_in[k], 16)

            sp.wait_ge(gu_ps, 1)
            for m in range(4):
                load_rows(m, m)
            with sp.Fori(1, R_TILES // 4) as r:
                for k in range(4):
                    sp.wait_ge(xT_ps, r * 4 + k - 3)
                    load_rows(r * 4 + k, k)

            for n in range(4):
                sp.wait_ge(ys_out[n], 16 * (R_TILES // 4))
            out_t = out.rearrange("b (t p) d -> p (b t) d", p=P)
            ys_t = ys_dram[0:TOP_K * TOK, :].rearrange("(t p k) d -> p t k d", p=P, k=TOP_K)
            x_t = x.rearrange("b (t p) d -> p (b t) d", p=P)

            def store(g):
                sp.wait_ge(summed, g + 1)
                t = slice(g * BACK, (g + 1) * BACK)
                sp.dma_start(out_t[:, t], s_sb[:, t.start * D:t.stop * D].rearrange("p (t d) -> p t d", d=D)).then_inc(stored, 16)

            for g in range(NT // BACK):
                if g >= BRING:
                    sp.wait_ge(summed, g - BRING + 1)
                sp.dma_start(back[:, g % BRING], ys_t[:, g * BACK:(g + 1) * BACK]).then_inc(back_in[g % BRING], 16)
                sp.dma_start(x_back[:, g % BRING], x_t[:, g * BACK:(g + 1) * BACK]).then_inc(back_in[g % BRING], 16)
                if g >= BRING:
                    store(g - BRING)
            for g in range(NT // BACK - BRING, NT // BACK):
                store(g)
            sp.wait_ge(stored, 16 * NT // BACK)

        @block.gpsimd
        def _(pool):
            pool.memset(s_sb[:], 0.0).then_inc(zeroed, 1)
            pool.memset(one[:], 1.0).then_inc(zeroed, 1)
            pool.memset(ones_b[:], 1.0).then_inc(zeroed, 1)
            for n, (dst, at, cols) in enumerate(W_CHUNKS):
                pool.wait_ge(w_hi, n + 1)
                pool.tensor_tensor(dst[1][:, at:at + cols], stage[:, n % NSTG * SCOLS:n % NSTG * SCOLS + cols], dst[0][:, at:at + cols], ALU.subtract).then_inc(w_lo, 1)
                if n == 1:
                    pool.wait_ge(const_in, 16 * 6)
                    pool.wait_ge(zeroed, 1)
                    pool.tensor_copy(fill[:, :, D + 1].bitcast(U32), row_id[:, TOP_K * NT:TOP_K * NT + FILL_TILES]).then_inc(filled, 1)

            def rotate_sum(name, item):
                buf = ROT_BUF[name]
                pool.wait_ge(misc_free, item)
                pool.tensor_tensor(rot_a[buf], rot_a[buf], rot_b[buf], ALU.add).then_inc(rot_add, 1)

            def rotate_lo(name, count):
                buf = ROT_BUF[name]
                dst = kT[1] if name == "k" else qT[1][:, int(name[1]) * S:(int(name[1]) + 1) * S]
                hi = kT[0] if name == "k" else qT[0][:, int(name[1]) * S:(int(name[1]) + 1) * S]
                pool.wait_ge(rot_hi, count)
                pool.tensor_tensor(dst, rot_a[buf], hi, ALU.subtract).then_inc(rot_lo, 1)

            def add_x(g):
                pool.wait_ge(gated, g + 1)
                cols = slice(g * BACK * D, (g + 1) * BACK * D)
                s = s_sb[:, cols].rearrange("p (t d) -> p t d", d=D)
                pool.tensor_tensor(s, s, x_back[:, g % BRING], ALU.add).then_inc(summed, 1)

            def divide(h, par):
                pool.wait_ge(inverted, h + 1)
                for qt in range(QT):
                    pr = probs[par][:, P_AT[qt]:P_AT[qt] + (qt + 1) * P]
                    ins = pool.tensor_tensor(pr, pr, rinv[:, par, qt:qt + 1].to_broadcast([P, (qt + 1) * P]), ALU.mult)
                ins.then_inc(normed, 1)

            for n, name in enumerate(ROT):
                rotate_sum(name, n + 1)
                rotate_lo(name, n + 1)
            divide(0, 0)

            def scatter(n, tiles_):
                for t in tiles_:
                    pool.indirect_dma_start(xs_dram, bass.IndirectOffsetOnAxis(slot_u[:, n, t:t + 1], 0),
                                            xn_t[:, t, :], None).then_inc((first_scattered, second_scattered)[n], 16)

            def shared_lo():
                pool.wait_ge(shared_hi, 2)
                for half in range(E_SHARED):
                    a, b = half * WE, half * WE + WG
                    pool.tensor_tensor(shared_s[1][:, a:b], stage[:, a:b], shared_s[0][:, a:b], ALU.subtract)
                    a, b = b, (half + 1) * WE
                    ins = pool.tensor_tensor(shared_s[1][0:HC, a:b], stage[0:HC, a:b], shared_s[0][0:HC, a:b], ALU.subtract)
                ins.then_inc(shared_w, 1)

            def round_(rd):
                for j in range(GH - 1):
                    if j > 0 and not rd.last:
                        rotate_sum(f"q{j - 1}", rd.item(f"q{j - 1}"))
                    divide(rd.head(j + 1), (j + 1) % 2)
                    if j > 0 and not rd.last:
                        rotate_lo(f"q{j - 1}", rd.rot(f"q{j - 1}"))
                    if rd.first and j == 1:
                        shared_lo()
                    if rd.last:
                        if j == 0:
                            pool.wait_ge(first_scattered, 16 * NT)
                            pool.tensor_copy(xn_t[:, :, D], weight[:, 1, :])
                            pool.tensor_copy(xn_t[:, :, D + 1].bitcast(U32), row_id[:, NT:2 * NT]).then_inc(second_meta, 1)
                            pool.wait_ge(second_meta, 1)
                        scatter(1, range(j * 5, j * 5 + 5))
                if rd.last:
                    scatter(1, range(15, NT))
                else:
                    for name in ("q2", "k"):
                        rotate_sum(name, rd.item(name))
                        rotate_lo(name, rd.rot(name))
                    rotate_sum("q3", rd.item("q3"))
                    divide(rd.head(GH), 0)
                    rotate_lo("q3", rd.rot("q3"))
                    if rd.first:
                        pool.wait_ge(xs_filled, 16 * FILLS)
                        pool.memset(fill[:, :, D + 1], 0.0).then_inc(zeroed, 1)
                        pool.wait_ge(slots_ready, 1)
                        scatter(0, range(NT))

            round_(Round(0, "first"))
            with pool.Fori(1, NG - 1) as i:
                round_(Round(i, "loop"))
            round_(Round(NG - 1, "last"))

            for e in range(0, E_ROUTED, 2):
                pool.wait_ge(expert_hi, e + 1)
                expert_lo(pool, e).then_inc(even_lo, 1)

            pool.wait_ge(meta_in, 16)
            for m in range(R_TILES):
                pool.wait_ge(ys_ready, m + 1)
                pool.indirect_dma_start(ys_dram, bass.IndirectOffsetOnAxis(meta[:, m, 1:2].bitcast(U32), 0),
                                        ys[:, m % 4, :], None).then_inc(ys_out[m % 4], 16)

            for g in range(NT // BACK):
                pool.wait_ge(back_in[g % BRING], 32 * (g // BRING + 1))
                pool.tensor_tensor(back[:, g % BRING, :, 0, :], back[:, g % BRING, :, 0, :], back[:, g % BRING, :, 1, :], ALU.add).then_inc(pair_sum, 1)
                if g >= 1:
                    add_x(g - 1)
            add_x(NT // BACK - 1)

        @block.scalar
        def _(act):
            act.dma_start(gate_f[:], gate_t.rearrange("(c p) e -> p c e", p=P)).then_inc(gate_in, 16)
            act.wait_ge(gate_in, 16)
            act.copy(gate_s[0][:], gate_f[:].rearrange("p c e -> p (c e)")).then_inc(const_cast, 1)
            act.wait_ge(const_in, 16 * 6)
            act.copy(ident_b[:], ident_f[:]).then_inc(const_cast, 1)
            act.copy(mask_b[:], mask_f).then_inc(const_cast, 1)
            act.copy(tri_b[:], tri_f).then_inc(const_cast, 1)
            act.wait_ge(var_ready, 1)
            act.activation(root[:], var[:], ACT.Sqrt).then_inc(rooted, 1)
            for n, (dst, at, cols) in enumerate(W_CHUNKS):
                act.wait_ge(stage_in[n], 32 if n == 0 else 16)
                act.copy(dst[0][:, at:at + cols], stage[:, n % NSTG * SCOLS:n % NSTG * SCOLS + cols]).then_inc(w_hi, 1)
                if n < B:
                    for c in range(KC):
                        act.wait_ge(xnT_ps, n * KC + c + 1)
                        act.copy(xnT[0][:, c * TOK + n * S:c * TOK + (n + 1) * S], xnT_bank[c][:]).then_inc(xnT_hi, 1)
            act.wait_ge(rt_shift, 1)
            act.activation(prob[:], prob[:], ACT.Exp).then_inc(rt_exp, 1)

            def rotate_hi(name, count):
                act.wait_ge(rot_add, count)
                dst = kT[0] if name == "k" else qT[0][:, int(name[1]) * S:(int(name[1]) + 1) * S]
                act.copy(dst, rot_a[ROT_BUF[name]]).then_inc(rot_hi, 1)

            def value_hi(rd):
                act.wait_ge(misc_ps, rd.item("v"))
                act.copy(v_s[0], misc_bank[rd.bank("v")][:]).then_inc(v_hi, 1)

            def exponentials(h, par, units=(0, 1, 2)):
                for u in units:
                    unit = SCORE_UNITS[u]
                    act.wait_ge(maxed, h * 3 + u + 1)
                    for qt, col in unit:
                        n = (qt + 1) * P
                        ins = act.activation(probs[par][:, P_AT[qt]:P_AT[qt] + n], score_bank[u][:, col:col + n], ACT.Exp,
                                             bias=nmax[:, par, qt:qt + 1], accum_out=rsum[:, par, qt:qt + 1])
                    ins.then_inc(exped, 1)

            def probs_hi(h, j, units):
                for u in units:
                    at, cols = PT_UNIT_COLS[u]
                    act.wait_ge(pt_ps, h * 3 + u + 1)
                    act.copy(pT[j % 2][0][:, at:at + cols], pt_bank[(3 * j + u) % 2][:, 0:cols]).then_inc(pt_hi, 1)

            def output_hi(rd, j):
                act.wait_ge(pv, rd.head(j) + 1)
                act.copy(oT[0][:, bass.ds((rd.i % 2) * (GH * S) + j * S, S)], o_bank[:]).then_inc(o_hi, 1)

            for n, name in enumerate(ROT):
                rotate_hi(name, n + 1)
            value_hi(PROLOGUE)
            exponentials(0, 0)

            def round_(rd):
                for j in range(GH - 1):
                    h, par = rd.head(j + 1), (j + 1) % 2
                    if j == 2:
                        output_hi(rd, 0)
                    exponentials(h, par, (0, 1))
                    probs_hi(rd.head(j), j, (0,))
                    exponentials(h, par, (2,))
                    probs_hi(rd.head(j), j, (1,))
                    if j > 0 and not rd.last:
                        rotate_hi(f"q{j - 1}", rd.rot(f"q{j - 1}"))
                    probs_hi(rd.head(j), j, (2,))
                    if rd.first and j == 1:
                        act.wait_ge(shared_in, 16 * (KC + 1) * E_SHARED)
                        for half in range(E_SHARED):
                            a, b = half * WE, half * WE + WG
                            act.copy(shared_s[0][:, a:b], stage[:, a:b])
                            a, b = b, (half + 1) * WE
                            act.copy(shared_s[0][0:HC, a:b], stage[0:HC, a:b]).then_inc(shared_hi, 1)
                output_hi(rd, 1)
                if not rd.last:
                    rotate_hi("q2", rd.rot("q2"))
                output_hi(rd, 2)
                probs_hi(rd.head(3), 3, (0, 1))
                if not rd.last:
                    rotate_hi("k", rd.rot("k"))
                probs_hi(rd.head(3), 3, (2,))
                if not rd.last:
                    exponentials(rd.head(GH), 0)
                output_hi(rd, 3)
                if not rd.last:
                    value_hi(rd)
                    rotate_hi("q3", rd.rot("q3"))

            round_(Round(0, "first"))
            with act.Fori(1, NG - 1) as i:
                round_(Round(i, "loop"))
            round_(Round(NG - 1, "last"))

            def expert_hi_part(e):
                act.wait_ge(expert_in[e % ERING], 32 * (e // ERING + 1))
                if e == 0:
                    act.wait_ge(misc_free, ATTENTION_ITEMS)
                at, st = e * WE, e % ERING * WE
                act.copy(expert_s[0][:, at:at + WG], stage[:, st:st + WG])
                act.copy(expert_s[0][0:HC, at + WG:at + WE], stage[0:HC, st + WG:st + WE]).then_inc(expert_hi, 1)

            def step(st):
                n = st.n
                if st.gu:
                    act.wait_ge(gu_ps, n + 1)
                    act.activation(sg[:, st.ring(2), :], gu_bank[st.ring(2)][:, 0:INTER], ACT.Silu).then_inc(silued, 1)
                if st.y and st.routed(LAG):
                    m = st.tile(LAG)
                    if st.like == SH_FIRST + LAG:
                        act.wait_ge(meta_in, 16)
                    act.wait_ge(down_ps, n - LAG + 1)
                    if st.like - LAG - SH_FIRST >= 4:
                        act.wait_ge(ys_out[st.ring(4, LAG)], stored_rows(st))
                    act.activation(ys[:, st.ring(4, LAG), :], y_bank[st.ring(2, LAG)][:, 0:D], ACT.Copy,
                                   scale=meta[:, bass.ds(m, 1), 0]).then_inc(ys_ready, 1)
                if st.t:
                    act.wait_ge(hT_ps, n)
                    act.copy(hT[0][:, st.ring(4, 1), :], hT_bank[st.ring(2, 1)][0:HC, 0:2 * P]).then_inc(hT_hi, 1)
                if st.rows:
                    act.wait_ge(xT_ps, st.tile(-2) + 1)
                    act.copy(xT[st.ring(2)][0], xT_bank[st.ring(2)][:, 0:KC * P]).then_inc(xT_hi, 1)
                if st.like == 0:
                    expert_hi_part(0)
                if st.like < E_ROUTED - 1:
                    expert_hi_part(st.like + 1)

            def stored_rows(st):
                m = st.tile(LAG)
                return (m - st.ring(4, LAG)) * 4

            ffn_steps(act, step)
            for g in range(NT // BACK):
                act.wait_ge(ffn_sum, g + 1)
                cols = slice(g * BACK * D, (g + 1) * BACK * D)
                act.activation(y_sb[:, cols], y_sb[:, cols], ACT.Silu).then_inc(gate_act, 1)

        @block.vector
        def _(dve):
            dve.wait_ge(const_cast, 1)
            dve.tensor_tensor(gate_s[1][:], gate_f[:].rearrange("p c e -> p (c e)"), gate_s[0][:], ALU.subtract).then_inc(ln_step, 1)
            dve.wait_ge(x_in, 16)
            for t in range(NT):
                dve.bn_stats(stats[:, t, :], x_sb[:, t * D:(t + 1) * D]).then_inc(ln_step, 1)
            dve.wait_ge(ln_step, NT + 1)
            for t in range(NT):
                dve.bn_aggr(mv[:, t, :], stats[:, t, :]).then_inc(ln_step, 1)
            dve.wait_ge(ln_step, 2 * NT + 1)
            dve.tensor_scalar(var[:], mv[:, :, 1], EPS, None, ALU.add).then_inc(var_ready, 1)
            dve.wait_ge(rooted, 1)
            dve.reciprocal(rstd[:], root[:]).then_inc(newton, 1)
            dve.wait_ge(newton, 1)
            dve.tensor_tensor(root[:], rstd[:], rstd[:], ALU.mult).then_inc(newton, 1)
            dve.wait_ge(newton, 2)
            dve.tensor_tensor(root[:], root[:], var[:], ALU.mult).then_inc(newton, 1)
            dve.wait_ge(newton, 3)
            dve.tensor_scalar(root[:], root[:], -0.5, 1.5, ALU.mult, ALU.add).then_inc(newton, 1)
            dve.wait_ge(newton, 4)
            dve.tensor_tensor(rstd[:], rstd[:], root[:], ALU.mult).then_inc(newton, 1)
            dve.wait_ge(newton, 5)
            for b in range(B):
                for q in range(QT):
                    t = b * QT + q
                    ins = dve.tensor_scalar(xn_t[:, t, 0:D], x_sb[:, t * D:(t + 1) * D], mv[:, t, 0:1], rstd[:, t:t + 1],
                                            ALU.subtract, ALU.mult)
                ins.then_inc(xn_ready, 1)
                for c in range(KC):
                    at = c * TOK + b * S
                    dve.wait_ge(xnT_hi, b * KC + c + 1)
                    dve.tensor_tensor(xnT[1][:, at:at + S], xnT_bank[c][:], xnT[0][:, at:at + S], ALU.subtract).then_inc(xnT_lo, 1)
            TE = [P, NT, E_ROUTED]

            def over_e(ap):
                return ap.rearrange("p (t o) -> p t o", o=1).to_broadcast(TE)

            def over_t(ap):
                return ap.rearrange("p (o e) -> p o e", o=1).to_broadcast(TE)

            chain = [0]

            def then(ins):
                chain[0] += 1
                ins.then_inc(rt, 1)
                dve.wait_ge(rt, chain[0])

            dve.wait_ge(logit_ps, 1)
            then(dve.tensor_copy(logit[:], logit_bank[:, 0:NT * E_ROUTED].rearrange("p (t e) -> p t e", e=E_ROUTED)))
            for t in range(NT):
                ins = dve.max(top[:, t, :], logit[:, t, :])
            then(ins)
            dve.tensor_tensor(prob[:], logit[:], top[:, :, 0:1].to_broadcast(TE), ALU.subtract).then_inc(rt_shift, 1)
            for t in range(NT):
                ins = dve.max_index(topi[:, t, :], top[:, t, :], logit[:, t, :])
            then(ins)
            then(dve.tensor_copy(topf[:], topi[:, :, 0:2]))
            dve.wait_ge(const_in, 16 * 6)
            for n in range(TOP_K):
                ins = dve.tensor_tensor(sel[n][:], over_t(iota_f[:, 0:E_ROUTED]), topf[:, :, n:n + 1].to_broadcast(TE), ALU.is_equal)
            then(ins)
            dve.tensor_tensor(sel_b[:].rearrange("p (t e) -> p t e", e=E_ROUTED), sel[0][:], sel[1][:], ALU.add).then_inc(chosen, 1)
            dve.wait_ge(rt_exp, 1)
            for n in range(TOP_K):
                dve.tensor_tensor(pick[n][:], sel[n][:], prob[:], ALU.mult)
            then(dve.tensor_reduce(zsum[:], prob[:], AX.X, ALU.add))
            for n in range(TOP_K):
                dve.tensor_reduce(weight[:, n, :], pick[n][:], AX.X, ALU.add)
            then(dve.reciprocal(zsum[:], zsum[:]))
            for n in range(TOP_K):
                ins = dve.tensor_tensor(weight[:, n, :], weight[:, n, :], zsum[:], ALU.mult)
            then(ins)
            dve.tensor_copy(xn_t[:, :, D], weight[:, 0, :])
            dve.tensor_copy(xn_t[:, :, D + 1].bitcast(U32), row_id[:, 0:NT])

            def place(part):
                if part == 0:
                    dve.wait_ge(rank_ps, 1)
                    ranks = rank_bank[:, 0:NT * E_ROUTED].rearrange("p (t e) -> p t e", e=E_ROUTED)
                    counts = rank_bank[:, NT * E_ROUTED:2 * NT * E_ROUTED].rearrange("p (t e) -> p e t", e=E_ROUTED)
                    then(dve.tensor_copy(count[:], counts))
                    flat = count[:].rearrange("p e t -> p (e t)")
                    then(dve.tensor_tensor_scan(total[:].rearrange("p e t -> p (e t)"), flat, flat, 0.0, ALU.add, ALU.max))
                    then(dve.tensor_tensor(count[:], total[:], count[:], ALU.subtract))
                    dve.tensor_tensor(slot[:], ranks, count[:].rearrange("p e t -> p t e"), ALU.add).then_inc(ranks_read, 1)
                if part == 1:
                    dve.memset(ends[:, 0:1], 0.0)
                    dve.tensor_scalar(steps128[:], iota_f[:, 0:E_ROUTED], float(P), None, ALU.mult)
                    then(dve.tensor_copy(ends[:, 1:E_ROUTED + 1], total[:, :, NT - 1]))
                    then(dve.tensor_tensor(held[:], ends[:, 1:E_ROUTED + 1], ends[:, 0:E_ROUTED], ALU.subtract))
                    EM = [P, E_ROUTED, E_ROUTED]
                    over = compare[:, 0:E_ROUTED * E_ROUTED].rearrange("p (e m) -> p e m", m=E_ROUTED)
                    then(dve.tensor_tensor(over, held[:].rearrange("p (e o) -> p e o", o=1).to_broadcast(EM),
                                           steps128[:].rearrange("p (o m) -> p o m", o=1).to_broadcast(EM), ALU.is_gt))
                    then(dve.tensor_reduce(tiles[:], over, AX.X, ALU.add))
                    then(dve.tensor_tensor_scan(tiles_to[:], tiles[:], tiles[:], 0.0, ALU.add, ALU.max))
                    then(dve.tensor_tensor(offset[:], tiles_to[:], tiles[:], ALU.subtract))
                if part == 2:
                    then(dve.scalar_tensor_tensor(out=offset[:], in0=offset[:], scalar=float(P), in1=ends[:, 0:E_ROUTED],
                                                  op0=ALU.mult, op1=ALU.subtract))
                    then(dve.tensor_tensor(slot[:], slot[:], over_t(offset[:]), ALU.add))
                    for n in range(TOP_K):
                        ins = dve.tensor_tensor(pick[n][:], sel[n][:], slot[:], ALU.mult)
                    then(ins)
                    for n in range(TOP_K):
                        ins = dve.tensor_reduce(slot_f[:, n, :], pick[n][:], AX.X, ALU.add)
                    then(ins)
                    dve.tensor_copy(slot_u[:], slot_f[:])
                if part == 3:
                    IE = [1, R_TILES, E_ROUTED]
                    before = compare[0:1, :].rearrange("p (i e) -> p i e", e=E_ROUTED)
                    then(dve.tensor_tensor(before, tiles_to[0:1, :].rearrange("p (o e) -> p o e", o=1).to_broadcast(IE),
                                           iota_f[0:1, :].rearrange("p (i o) -> p i o", o=1).to_broadcast(IE), ALU.is_le))
                    then(dve.tensor_reduce(tile_e[:], before, AX.X, ALU.add))
                    then(dve.tensor_scalar(tile_e[:], tile_e[:], float(E_ROUTED - 1), None, ALU.min))
                    dve.tensor_copy(tile_u[:], tile_e[:]).then_inc(slots_ready, 1)

            def rotate_products(name, item, bank_n, freed):
                ps, buf = misc_bank[bank_n], ROT_BUF[name]
                cos, sin = (2, 3) if name == "k" else (0, 1)
                dve.wait_ge(misc_ps, item)
                if freed is not None:
                    dve.wait_ge(rot_lo, freed)
                dve.tensor_tensor(rot_a[buf], ps[:], tab[:, cos, :], ALU.mult)
                half = DH // 2
                dve.tensor_tensor(rot_b[buf][0:half, :], ps[half:DH, :], tab[half:DH, sin, :], ALU.mult)
                dve.tensor_tensor(rot_b[buf][half:DH, :], ps[0:half, :], tab[0:half, sin, :], ALU.mult).then_inc(misc_free, 1)

            def value_lo(rd):
                dve.wait_ge(v_hi, rd.i + 2)
                dve.tensor_tensor(v_s[1], misc_bank[rd.bank("v")][:], v_s[0], ALU.subtract).then_inc(misc_free, 1)

            def row_max(h, par, units=(0, 1, 2)):
                for u in units:
                    unit = SCORE_UNITS[u]
                    dve.wait_ge(scores, h * 3 + u + 1)
                    for qt, col in unit:
                        ins = dve.tensor_reduce(nmax[:, par, qt:qt + 1], score_bank[u][:, col:col + (qt + 1) * P], AX.X, ALU.max, negate=True)
                    ins.then_inc(maxed, 1)

            def invert_sums(h, par):
                dve.wait_ge(exped, h * 3 + 3)
                dve.reciprocal(rinv[:, par, :], rsum[:, par, :]).then_inc(inverted, 1)

            def probs_lo(h, j, units):
                for u in units:
                    at, cols = PT_UNIT_COLS[u]
                    dve.wait_ge(pt_hi, h * 3 + u + 1)
                    dve.tensor_tensor(pT[j % 2][1][:, at:at + cols], pt_bank[(3 * j + u) % 2][:, 0:cols], pT[j % 2][0][:, at:at + cols],
                                      ALU.subtract).then_inc(pt_lo, 1)

            def output_lo(rd, j):
                dve.wait_ge(o_hi, rd.head(j) + 1)
                cols = bass.ds((rd.i % 2) * (GH * S) + j * S, S)
                dve.tensor_tensor(oT[1][:, cols], o_bank[:], oT[0][:, cols], ALU.subtract).then_inc(o_lo, 1)

            def add_projection(rd, q):
                at = ((rd.i - 1) // NKV) * (QT * D) + q * D
                dve.wait_ge(misc_ps, rd.item(f"o{q}"))
                dve.wait_ge(misc_free, rd.item(f"o{q}") - 4)
                dve.tensor_tensor(s_sb[:, bass.ds(at, D)], misc_bank[rd.bank(f"o{q}")][:, 0:D], s_sb[:, bass.ds(at, D)],
                                  ALU.add).then_inc(misc_free, 1)

            for n, name in enumerate(ROT):
                rotate_products(name, PROLOGUE.item(name), PROLOGUE.bank(name), {2: 1, 4: 2}.get(n))
            value_lo(PROLOGUE)
            row_max(0, 0)
            invert_sums(0, 0)

            def round_(rd):
                i = rd.i
                freed = {"q0": i * 5 + 3, "q1": i * 5 + 5, "q2": i * 5 + 6, "k": i * 5 + 4, "q3": i * 5 + 7}

                def rope(name):
                    if not rd.last:
                        rotate_products(name, rd.item(name), rd.bank(name), freed[name])

                for j in range(GH - 1):
                    h, par = rd.head(j + 1), (j + 1) % 2
                    row_max(h, par, (0,))
                    if j == 2:
                        output_lo(rd, 0)
                    row_max(h, par, (1, 2))
                    probs_lo(rd.head(j), j, (0,))
                    invert_sums(h, par)
                    probs_lo(rd.head(j), j, (1,))
                    rope(f"q{j}")
                    if not rd.first:
                        add_projection(rd, j)
                    probs_lo(rd.head(j), j, (2,))
                    if rd.first:
                        place(j)
                output_lo(rd, 1)
                rope("k")
                output_lo(rd, 2)
                probs_lo(rd.head(3), 3, (0, 1))
                rope("q3")
                probs_lo(rd.head(3), 3, (2,))
                if rd.first:
                    place(3)
                else:
                    add_projection(rd, 3)
                if not rd.last:
                    row_max(rd.head(GH), 0)
                output_lo(rd, 3)
                if not rd.last:
                    invert_sums(rd.head(GH), 0)
                    value_lo(rd)

            round_(Round(0, "first"))
            dve.wait_ge(zeroed, 4)
            with dve.Fori(1, NG - 1) as i:
                round_(Round(i, "loop"))
            round_(Round(NG - 1, "last"))
            for q in range(QT):
                add_projection(EPILOGUE, q)

            def step(st):
                n = st.n
                if st.gu:
                    dve.wait_ge(silued, n + 1)
                    dve.tensor_tensor(hid[:, st.ring(2), :], gu_bank[st.ring(2)][:, INTER:GU], sg[:, st.ring(2), :], ALU.mult).then_inc(hidden, 1)
                if st.y and not st.routed(LAG):
                    d = st.tile(LAG)
                    yt = y_sb[:, bass.ds((d % NT) * D, D)]
                    if st.like == LAG:
                        dve.wait_ge(second_scattered, 16 * NT)
                    dve.wait_ge(down_ps, n - LAG + 1)
                    ps = y_bank[st.ring(2, LAG)][:, 0:D]
                    if st.like - LAG < NT:
                        dve.tensor_copy(yt, ps).then_inc(y_done, 1)
                    else:
                        dve.wait_ge(y_done, d - NT + 1)
                        dve.tensor_tensor(yt, yt, ps, ALU.add).then_inc(y_done, 1)
                if st.t:
                    dve.wait_ge(hT_hi, n)
                    dve.tensor_tensor(hT[1][:, st.ring(4, 1), :], hT_bank[st.ring(2, 1)][0:HC, 0:2 * P], hT[0][:, st.ring(4, 1), :],
                                      ALU.subtract).then_inc(hT_lo, 1)
                if st.rows:
                    dve.wait_ge(xT_hi, st.tile(-2) + 1)
                    dve.tensor_tensor(xT[st.ring(2)][1], xT_bank[st.ring(2)][:, 0:KC * P], xT[st.ring(2)][0], ALU.subtract).then_inc(xT_lo, 1)
                if st.like < E_ROUTED and st.like % 2:
                    dve.wait_ge(expert_hi, st.like + 1)
                    expert_lo(dve, st.like).then_inc(odd_lo, 1)

            ffn_steps(dve, step)
            for g in range(NT // BACK + 1):
                if g < NT // BACK:
                    cols = slice(g * BACK * D, (g + 1) * BACK * D)
                    if g == 0:
                        dve.wait_ge(y_done, SH_STEPS)
                    dve.wait_ge(pair_sum, g + 1)
                    dve.tensor_tensor(y_sb[:, cols].rearrange("p (t d) -> p t d", d=D), y_sb[:, cols].rearrange("p (t d) -> p t d", d=D),
                                      back[:, g % BRING, :, 0, :], ALU.add).then_inc(ffn_sum, 1)
                if g >= 1:
                    cols = slice((g - 1) * BACK * D, g * BACK * D)
                    dve.wait_ge(gate_act, g)
                    if g == 1:
                        dve.wait_ge(misc_free, ATTENTION_ITEMS)
                    dve.tensor_tensor(s_sb[:, cols], s_sb[:, cols], y_sb[:, cols], ALU.mult).then_inc(gated, 1)

        @block.tensor
        def _(pe):
            pe.wait_ge(const_in, 16 * 6)
            for b in range(B):
                pe.wait_ge(xn_ready, b + 1)
                for c in range(KC):
                    if b >= 1:
                        pe.wait_ge(xnT_lo, (b - 1) * KC + c + 1)
                    for q in range(QT):
                        ins = pe.transpose(xnT_bank[c][:, q * P:(q + 1) * P], xn_t[:, b * QT + q, c * P:(c + 1) * P], ident_f[:])
                    ins.then_inc(xnT_ps, 1)
            pe.wait_ge(xnT_lo, B * KC)
            pe.wait_ge(ln_step, 1)
            for t in range(NT):
                for c in range(KC):
                    for n, (a, m) in enumerate(PASSES):
                        ins = pe.matmul(logit_bank[:, t * E_ROUTED:(t + 1) * E_ROUTED], xnT[a][:, c * TOK + t * P:c * TOK + (t + 1) * P],
                                        gate_s[m][:, c * E_ROUTED:(c + 1) * E_ROUTED],
                                        start=(c == 0 and n == 0), stop=(c == KC - 1 and n == 2))
            ins.then_inc(logit_ps, 1)

            def project(rd, name):
                i, item, ps = rd.i + 1, rd.item(name), misc_bank[rd.bank(name)]
                b, g = i // NKV, i % NKV
                if not (rd is PROLOGUE and item <= 2):
                    pe.wait_ge(misc_free, item - 2)
                for c in range(KC):
                    for n, (a, m) in enumerate(PASSES):
                        if name == "k":
                            w = wkv_s[a][:, bass.ds(c * 512 + g * DH, DH)]
                        else:
                            w = wq_s[a][:, bass.ds(c * 2048 + g * (GH * DH) + int(name[1]) * DH, DH)]
                        ins = pe.matmul(ps[:], w, xnT[m][:, bass.ds(c * TOK + b * S, S)], start=(c == 0 and n == 0), stop=(c == KC - 1 and n == 2))
                ins.then_inc(misc_ps, 1)

            def project_values(rd):
                i, item, ps = rd.i + 1, rd.item("v"), misc_bank[rd.bank("v")]
                b, g = i // NKV, i % NKV
                pe.wait_ge(misc_free, item - 2)
                for q in range(QT):
                    for c in range(KC):
                        for n, (a, m) in enumerate(PASSES):
                            ins = pe.matmul(ps[:, q * DH:(q + 1) * DH], xnT[a][:, bass.ds(c * TOK + b * S + q * P, P)],
                                            wkv_s[m][:, bass.ds(1024 + c * 512 + g * DH, DH)],
                                            start=(c == 0 and n == 0), stop=(c == KC - 1 and n == 2))
                ins.then_inc(misc_ps, 1)

            def score(h, j, queries, keys, reuse):
                pe.wait_ge(rot_lo, queries)
                if keys is not None:
                    pe.wait_ge(rot_lo, keys)
                for u, unit in enumerate(SCORE_UNITS):
                    if reuse:
                        pe.wait_ge(exped, h * 3 + u - 2)
                    for qt, col in unit:
                        n_k = (qt + 1) * P
                        for n, (a, m) in enumerate(PASSES):
                            pe.matmul(score_bank[u][:, col:col + n_k], qT[a][:, j * S + qt * P:j * S + (qt + 1) * P], kT[m][:, 0:n_k],
                                      start=(n == 0), stop=False)
                        ins = pe.matmul(score_bank[u][:, col + qt * P:col + n_k], ident_b[:], mask_b[:], start=False, stop=True)
                    ins.then_inc(scores, 1)

            def transpose_probs(h, j, units):
                for u in units:
                    if u == 0:
                        pe.wait_ge(normed, h + 1)
                    if not (j == 0 and u < 2):
                        pe.wait_ge(pt_lo, h * 3 + u - 1)
                    for kt, col in PT_UNITS[u]:
                        for qt in range(kt, QT):
                            ins = pe.transpose(pt_bank[(3 * j + u) % 2][:, col + (qt - kt) * P:col + (qt - kt + 1) * P],
                                               probs[j % 2][:, P_AT[qt] + kt * P:P_AT[qt] + (kt + 1) * P], ident_f[:])
                    ins.then_inc(pt_ps, 1)

            def weigh_values(rd, j):
                h = rd.head(j)
                if j == 0:
                    pe.wait_ge(misc_free, rd.base)
                    if rd.first:
                        pe.wait_ge(ranks_read, 1)
                if j > 0 or not rd.first:
                    pe.wait_ge(o_lo, h)
                for kt in (0, 1, 3, 2):
                    n_q = (QT - kt) * P
                    if kt != 3:
                        pe.wait_ge(pt_lo, h * 3 + kt + 1)
                    for n, (a, m) in enumerate(PASSES):
                        ins = pe.matmul(o_bank[:, kt * P:S], v_s[a][:, kt * DH:(kt + 1) * DH], pT[j % 2][m][:, PT_AT[kt]:PT_AT[kt] + n_q],
                                        start=(kt == 0 and n == 0), stop=(kt == 2 and n == 2))
                ins.then_inc(pv, 1)

            def project_out(rd, q):
                i, item, ps = rd.i - 1, rd.item(f"o{q}"), misc_bank[rd.bank(f"o{q}")]
                pe.wait_ge(o_lo, rd.i * GH)
                pe.wait_ge(misc_free, item - 2)
                for j in range(GH):
                    for n, (a, m) in enumerate(PASSES):
                        ins = pe.matmul(ps[:, 0:D], oT[a][:, bass.ds((i % 2) * (GH * S) + j * S + q * P, P)],
                                        wo_s[m][:, bass.ds((i % NKV) * (GH * D) + j * D, D)],
                                        start=(j == 0 and n == 0), stop=(j == GH - 1 and n == 2))
                ins.then_inc(misc_ps, 1)

            pe.wait_ge(w_lo, N_CHUNKS)
            pe.wait_ge(const_cast, 4)
            for name in ROT:
                project(PROLOGUE, name)
            project_values(PROLOGUE)
            pe.wait_ge(chosen, 1)
            pe.wait_ge(zeroed, 3)
            pe.matmul(rank_bank[:, 0:NT * E_ROUTED], tri_b[:], sel_b[:], start=True, stop=True)
            pe.matmul(rank_bank[:, NT * E_ROUTED:2 * NT * E_ROUTED], ones_b[:], sel_b[:], start=True, stop=True).then_inc(rank_ps, 1)
            score(0, 0, 1, 4, False)

            def round_(rd):
                queries = [rd.i * 5 + n for n in (1, 2, 3, 5)]
                for j in range(GH - 1):
                    h = rd.head(j)
                    score(h + 1, j + 1, queries[j + 1], None, True)
                    transpose_probs(h, j, (0, 1))
                    if not rd.last:
                        project(rd, f"q{j}")
                    if not rd.first:
                        project_out(rd, j)
                    transpose_probs(h, j, (2,))
                    if j >= 1:
                        weigh_values(rd, j - 1)
                if not rd.last:
                    project(rd, "k")
                weigh_values(rd, 2)
                transpose_probs(rd.head(3), 3, (0, 1))
                if not rd.last:
                    project(rd, "q3")
                transpose_probs(rd.head(3), 3, (2,))
                if not rd.first:
                    project_out(rd, 3)
                if not rd.last:
                    score(rd.head(GH), 0, rd.rot("q0"), rd.rot("k"), True)
                weigh_values(rd, 3)
                if not rd.last:
                    project_values(rd)

            round_(Round(0, "first"))
            with pe.Fori(1, NG - 1) as i:
                round_(Round(i, "loop"))
            round_(Round(NG - 1, "last"))
            for q in range(QT):
                project_out(EPILOGUE, q)

            def expert_of(m):
                return pe.value_load(tile_u[0:1, bass.ds(m, 1)], min_val=0, max_val=E_ROUTED - 1)

            def step(st):
                n = st.n
                if st.gu:
                    gu = gu_bank[st.ring(2)][:, 0:GU]
                    if st.like == 0:
                        pe.wait_ge(shared_w, 1)
                    if st.like >= 2:
                        pe.wait_ge(hidden, n - 1)
                    if st.routed():
                        if st.like == SH_FIRST:
                            pe.wait_ge(even_lo, E_ROUTED // 2)
                            pe.wait_ge(odd_lo, E_ROUTED // 2)
                        m = st.tile()
                        w = expert_of(m) * WE
                        pe.wait_ge(xT_lo, m + 1)
                    for c in range(KC):
                        for p, (a, b) in enumerate(PASSES):
                            if st.routed():
                                rows_, cols = xT[st.ring(2)][a][:, c * P:(c + 1) * P], expert_s[b][:, bass.ds(w + c * GU, GU)]
                            else:
                                half, t = st.tile() // NT, st.tile() % NT
                                rows_ = xnT[a][:, bass.ds(c * TOK + t * P, P)]
                                cols = shared_s[b][:, bass.ds(half * WE + c * GU, GU)]
                            ins = pe.matmul(gu, rows_, cols, start=(c == 0 and p == 0), stop=(c == KC - 1 and p == 2))
                    ins.then_inc(gu_ps, 1)
                if st.y:
                    if st.routed(LAG):
                        w = expert_of(st.tile(LAG)) * WE + WG
                    else:
                        w = (st.tile(LAG) // NT) * WE + WG
                    w_s = expert_s if st.routed(LAG) else shared_s
                    pe.wait_ge(hT_lo, n - LAG + 1)
                    if st.like >= LAG + 2:
                        pe.wait_ge(ys_ready if st.routed(LAG + 2) else y_done, st.tile(LAG + 2) + 1)
                    for c in range(2):
                        for p, (a, b) in enumerate(PASSES):
                            ins = pe.matmul(y_bank[st.ring(2, LAG)][:, 0:D], hT[a][:, st.ring(4, LAG), c * P:(c + 1) * P],
                                            w_s[b][0:HC, bass.ds(w + c * D, D)],
                                            start=(c == 0 and p == 0), stop=(c == 1 and p == 2))
                    ins.then_inc(down_ps, 1)
                if st.t:
                    pe.wait_ge(hidden, n)
                    if st.like >= 3:
                        pe.wait_ge(hT_lo, n - 2)
                    for c in range(2):
                        ins = pe.transpose(hT_bank[st.ring(2, 1)][0:HC, c * P:(c + 1) * P], hid[:, st.ring(2, 1), c * HC:(c + 1) * HC], ident_f[:])
                    ins.then_inc(hT_ps, 1)
                if st.rows:
                    m = st.tile(-2)
                    if st.like + 2 == SH_FIRST:
                        pe.wait_ge(misc_free, ATTENTION_ITEMS)
                    pe.wait_ge(xs_in[st.ring(4, -2)], (m - st.ring(4, -2)) * 4 + 16)
                    if st.like + 2 >= SH_FIRST + 2:
                        pe.wait_ge(xT_lo, m - 1)
                    for c in range(KC):
                        ins = pe.transpose(xT_bank[st.ring(2)][:, c * P:(c + 1) * P], xs[:, st.ring(4, -2), c * P:(c + 1) * P], ident_f[:])
                    ins.then_inc(xT_ps, 1)

            pe.wait_ge(slots_ready, 1)
            ffn_steps(pe, step)


def kernel(**inputs):
    import numpy as np
    import concourse.bacc as bacc
    from concourse.bass_utils import run_bass_kernel_spmd

    pos = np.arange(S, dtype=np.float32)
    half = DH // 2
    inv_freq = (1.0 / 10000.0 ** (np.arange(half, dtype=np.float32) / np.float32(half))).astype(np.float32)
    freqs = np.outer(pos, inv_freq).astype(np.float32)
    cos = np.cos(np.concatenate([freqs, freqs], -1)).astype(np.float64)
    sin = np.sin(np.concatenate([freqs, freqs], -1)).astype(np.float64)
    scale = (pos.astype(np.float64) + 32.0) / 64.0
    xs = np.stack([np.repeat(scale[:, None], half, 1), np.repeat(1.0 / scale[:, None], half, 1)], -1).reshape(S, DH)
    sgn = np.concatenate([-np.ones(half), np.ones(half)])
    qs, ks = xs / np.sqrt(DH), 1.0 / xs
    tables = [cos * qs, np.roll(sin * sgn * qs, -half, 1), cos * ks, np.roll(sin * sgn * ks, -half, 1)]
    rope = np.ascontiguousarray(np.stack([t.T for t in tables]).astype(np.float32))

    token = np.arange(NT)[None, None] * P + np.arange(P)[:, None, None]
    rows = (TOP_K * token + np.arange(TOP_K)[None, :, None]).reshape(P, TOP_K * NT)
    empty = TOP_K * TOK + np.arange(R_TILES)[None] * P + np.arange(P)[:, None]
    rows = np.concatenate([rows, empty], 1).astype(np.float32)

    arrays = {
        "x": inputs["L0_attn_x"], "wq": inputs["L0_attn_Wq"], "wk": inputs["L0_attn_Wk"], "wv": inputs["L0_attn_Wv"],
        "wo": inputs["L0_attn_Wo"], "gate_t": np.asarray(inputs["L0_ffn_gate_w"]).T, "w_gate_up": inputs["L0_ffn_w_gate_up"],
        "w_down": inputs["L0_ffn_w_down"], "shared_gu": inputs["L0_ffn_shared_gate_up"], "shared_down": inputs["L0_ffn_shared_down"],
        "rope": rope, "ident": np.eye(P, dtype=np.float32),
        "mask": np.where(np.tril(np.ones((P, P), bool)), 0.0, -1e30).astype(np.float32),
        "iota": np.tile(np.arange(R_TILES, dtype=np.float32), (P, 1)), "tri": np.triu(np.ones((P, P), np.float32), 1),
        "rows": rows,
    }
    arrays = {n: np.ascontiguousarray(a) for n, a in arrays.items()}
    nc = bacc.Bacc("TRN2", target_bir_lowering=False, num_devices=1)
    aps = [nc.dram_tensor(n, a.shape, mybir.dt.from_np(a.dtype), kind="ExternalInput").ap() for n, a in arrays.items()]
    aps.append(nc.dram_tensor("out", (B, S, D), F32, kind="ExternalOutput").ap())
    build(nc, *aps)
    return run_bass_kernel_spmd(nc, [arrays], core_ids=[0]).results[0]["out"]
```

```python
from contextlib import ExitStack

import concourse.bass as bass
from concourse import mybir

F32 = mybir.dt.float32
F16 = mybir.dt.float16
BF16 = mybir.dt.bfloat16
U32 = mybir.dt.uint32
ACT = mybir.ActivationFunctionType
ALU = mybir.AluOpType
AX = mybir.AxisListType

P = 128
B, S, D = 4, 512, 256
KC = D // P
TOK = B * S
NT = TOK // P
QT = S // P
NH, NKV, DH = 16, 4, 128
GH = NH // NKV
NG = B * NKV
E_ROUTED, INTER, TOP_K = 16, 176, 2
E_SHARED = 2
HC = INTER // 2
GU = 2 * INTER
WG, WD = KC * GU, 2 * D
WE = WG + WD
SHARED_ROWS = [min(P, E_SHARED * INTER - c * P) for c in range(-(-E_SHARED * INTER // P))]
SHARED_WG = E_SHARED * WG
SHARED_W = SHARED_WG + len(SHARED_ROWS) * D
assert SHARED_W <= E_SHARED * WE and len(SHARED_ROWS) <= 4 and SHARED_ROWS[:-1] == [P] * (len(SHARED_ROWS) - 1)
R_TILES = (TOP_K * TOK + E_ROUTED * (P - 1)) // P
R_TILES = -(-R_TILES // 4) * 4
DX = D + 2
SH_STEPS = E_SHARED * NT
SH_FIRST = 16
SH_TILES = SH_FIRST // E_SHARED
BODY = 8
ROUTED_END = SH_FIRST + R_TILES
STEPS = SH_STEPS + R_TILES
FILLS = 4
GROUP = 4
BACK = 2
GROUPS = NT // BACK
EARLY = 5
LAG = 2
assert E_ROUTED ** (GROUP + LAG) <= 2 ** 24
EPS = 1e-5

SCORE_UNITS = [[(3, 0)], [(2, 0), (0, 384)], [(1, 0)]]
PT_UNITS = [[(0, 0)], [(1, 0), (3, 384)], [(2, 0)]]
PT_AT = {0: 0, 1: 512, 3: 896, 2: 1024}
PT_UNIT_COLS = [(0, 512), (512, 512), (1024, 256)]
P_AT = [0, 128, 384, 768]
PCOLS = 1280

ITEMS_PROLOGUE = ["q0", "k", "q1", "q2", "q3"]
ITEMS_FIRST = ["q0", "v", "x10", "q1", "x11", "x20", "k", "x21", "x30", "q2", "x31", "q3", "logit"]
ITEMS_SECOND = ["q0", "v", "q1", "o0", "k", "o1", "rank", "q2", "o2", "q3", "o3"]
ITEMS_LOOP = ["q0", "v", "q1", "o0", "k", "o1", "q2", "o2", "q3", "o3"]
ITEMS_LAST = ["v", "o0", "o1", "o2", "o3"]
ITEMS_EPILOGUE = ["o0", "o1", "o2", "o3"]
X_BEFORE = [[], ["x10"], ["x20"]]
X_AFTER = [[], ["x11"], ["x21", "x30"], ["x31"]]
ROT = ["q0", "q1", "k", "q2", "q3"]
ROT_BUF = {"q0": 0, "q1": 1, "q2": 0, "k": 2, "q3": 1}
ROT_BUF_PROLOGUE = {**ROT_BUF, "q2": 2}


class Round:

    def __init__(self, i, kind):
        self.i, self.first, self.last = i, kind == "first", kind == "last"
        self.prologue = kind == "prologue"
        self.second, self.third = kind == "second", kind == "third"
        self.early = self.first or self.second or self.third
        self.items = {"prologue": ITEMS_PROLOGUE, "first": ITEMS_FIRST, "second": ITEMS_SECOND, "third": ITEMS_LOOP,
                      "loop": ITEMS_LOOP, "last": ITEMS_LAST, "epilogue": ITEMS_EPILOGUE}[kind]
        loop, start = len(ITEMS_LOOP), {"prologue": 0, "first": len(ITEMS_PROLOGUE)}
        start["second"] = start["first"] + len(ITEMS_FIRST)
        start["third"] = start["loop"] = start["second"] + len(ITEMS_SECOND)
        start["last"] = start["loop"] + loop * (NG - 3)
        start["epilogue"] = start["last"] + len(ITEMS_LAST)
        self.base = (i - 2) * loop + start[kind] if kind == "loop" else start[kind]
        self.odd = start[kind] % 2

    def item(self, name):
        return self.base + self.items.index(name) + 1

    def bank(self, name):
        return (self.odd + self.items.index(name)) % 2

    def head(self, j):
        return self.i * GH + j

    def tile(self):
        return None if self.early else self.i - 2

    def rot(self, name):
        return (self.i + 1) * len(ROT) + (ITEMS_PROLOGUE if self.prologue else ROT).index(name) + 1


assert len(ITEMS_LOOP) % 2 == 0
PROLOGUE, EPILOGUE = Round(-1, "prologue"), Round(NG, "epilogue")
ATTENTION_ITEMS = EPILOGUE.base + len(ITEMS_EPILOGUE)


class Step:

    def __init__(self, n, like):
        self.n, self.like = n, like
        self.gu = like < STEPS
        self.t = self.projects(1)
        self.y = self.projects(LAG)
        self.rows = SH_FIRST <= like + 2 < ROUTED_END
        first = STEPS - BACK * EARLY
        self.out = (like - first) // BACK if like >= first and like < STEPS and (like - first) % BACK == BACK - 1 else None

    def projects(self, back):
        m = self.like - back
        return 0 <= m < STEPS and (self.routed(back) or m % E_SHARED == E_SHARED - 1)

    def layers(self, back):
        if self.routed(back):
            return self.n - (back + SH_FIRST - SH_TILES - 1)
        m = self.like - back
        return (m + 1) // E_SHARED if m < SH_FIRST else SH_TILES + R_TILES + (m + 1 - ROUTED_END) // E_SHARED

    def parity(self, back):
        m = self.like - back
        return (m - SH_FIRST + SH_TILES + 1 if self.routed(back) else self.layers(back)) % 2

    def routed(self, back=0):
        return SH_FIRST <= self.like - back < ROUTED_END

    def tile(self, back=0):
        if self.routed(back):
            return self.n - (back + SH_FIRST)
        return (self.n - back if self.like - back < SH_FIRST else self.n - (back + R_TILES)) // E_SHARED

    def pair(self, back):
        return self.ring(4, back) - (E_SHARED - 1)

    def ring(self, of, back=0):
        return (self.like - back) % of


def ffn_steps(engine, step):
    lo, hi = SH_FIRST + 8, (ROUTED_END - 2) // BODY * BODY
    for n in range(lo):
        step(Step(n, n))
    with engine.Fori(lo // BODY, hi // BODY) as r:
        for k in range(BODY):
            step(Step(r * BODY + k, lo + k))
    for n in range(hi, STEPS):
        step(Step(n, n))
    for n in range(STEPS, STEPS + LAG):
        step(Step(n, n))


def build(nc, x, wq, wk, wv, wo, gate_t, w_gate_up, w_down, shared_gu, shared_down, rope, ident, mask, iota, tri, rows, digits, out):
    with ExitStack() as ctx:
        def sb(name, shape, dt):
            return ctx.enter_context(nc.sbuf_tensor(name, shape, dt))

        def sem(name):
            return ctx.enter_context(nc.semaphore(name))

        ident_f = sb("ident_f", [P, P], F32)
        ident_b = sb("ident_b", [P, P], BF16)
        mask_b = sb("mask_b", [P, S], BF16)
        tri_b = sb("tri_b", [P, P], BF16)
        ones_b = sb("ones_b", [P, P], BF16)
        one = sb("one", [P, 1], F32)
        iota_f = sb("iota_f", [P, R_TILES], F32)
        digit = sb("digit", [1, R_TILES], F32)
        tab = sb("tab", [P, 4, S], F32)
        s_sb = sb("s_sb", [P, NT * D], F32)
        row_id = sb("row_id", [P, TOP_K * NT + R_TILES // FILLS], F32)
        xn = sb("xn", [P, NT * D], F32)
        xn_t = xn[:].rearrange("p (t d) -> p t d", d=D)
        y_sb = xn
        xnT = [sb("xnT_hi", [P, KC * TOK], F16), sb("xnT_lo", [P, KC * TOK], BF16)]
        stats = sb("stats", [P, NT, 6], F32)
        mv = sb("mv", [P, NT, 2], F32)
        rstd = sb("rstd", [P, NT], F32)
        var = sb("var", [P, NT], F32)
        root = sb("root", [P, NT], F32)
        shift = root
        gate_f = sb("gate_f", [P, KC, E_ROUTED], F32)
        gate_s = [sb("gate_hi", [P, KC * E_ROUTED], F16), sb("gate_lo", [P, KC * E_ROUTED], BF16)]
        logit = sb("logit", [P, NT, E_ROUTED], F32)
        top = sb("top", [P, NT, 8], F32)
        topi = sb("topi", [P, NT, 8], U32)
        topf = sb("topf", [P, NT, 2], F32)
        sel = [sb(f"sel{n}", [P, NT, E_ROUTED], F32) for n in range(TOP_K)]
        sel_b = sb("sel_b", [P, NT * E_ROUTED], BF16)
        prob = sb("prob", [P, NT, E_ROUTED], F32)
        pick = [sb(f"pick{n}", [P, NT, E_ROUTED], F32) for n in range(TOP_K)]
        zsum = sb("zsum", [P, NT], F32)
        weight = sb("weight", [P, NT], F32)
        total = sb("total", [P, E_ROUTED, NT], F32)
        ends = sb("ends", [P, E_ROUTED + 1], F32)
        held = sb("held", [P, E_ROUTED], F32)
        steps128 = sb("steps128", [P, E_ROUTED], F32)
        compare = sb("compare", [P, R_TILES * E_ROUTED], F32)
        count = compare[:, E_ROUTED * E_ROUTED:E_ROUTED * (E_ROUTED + NT)].rearrange("p (e t) -> p e t", t=NT)
        mask_f, tri_f = compare[:, 0:P], compare[:, P:2 * P]
        rows_out = compare[:, 0:TOP_K * DX].rearrange("p (n d) -> p n d", d=DX)
        slot_now = sb("slot_now", [P, TOP_K], U32)
        slot_to = sb("slot_to", [P, NT, TOP_K], F32)
        tags = sb("tags", [P, NT, TOP_K, 2], F32)
        tiles = sb("tiles", [P, E_ROUTED], F32)
        tiles_to = sb("tiles_to", [P, E_ROUTED], F32)
        offset = sb("offset", [P, E_ROUTED], F32)
        slot = logit
        tile_e = sb("tile_e", [1, R_TILES], F32)
        group_e = sb("group_e", [1, R_TILES // GROUP], F32)
        group_u = sb("group_u", [1, R_TILES // GROUP], U32)
        meta = sb("meta", [P, R_TILES, 2], F32)
        row_u = sb("row_u", [P, R_TILES], U32)
        NSTG, SCOLS = 6, 1024
        stage = sb("stage", [P, NSTG * SCOLS], F32)
        ERING = 5
        shared_s = [sb("shared_hi", [P, SHARED_W], F16), sb("shared_lo", [P, SHARED_W], BF16)]

        ARENA = 102400
        arena = sb("arena", [P, ARENA // 4], F32)
        taken = [0]

        def carve(cols, dt):
            size = 4 if dt == F32 else 2
            a = taken[0]
            taken[0] = a + cols * size // 4
            assert taken[0] * 4 <= ARENA
            return arena[:, a:taken[0]] if dt == F32 else arena[:, a:taken[0]].bitcast(dt)

        def split(cols):
            return [carve(cols, F16), carve(cols, BF16)]

        wkv_s, wq_s, wo_s = split(2 * KC * 512), split(KC * 2048), split(NH * D)
        qT, kT, v_s = split(GH * S), split(S), split(S)
        rot_a = [carve(S, F32) for _ in range(3)]
        rot_b = [carve(S, F32) for _ in range(3)]
        probs = [carve(PCOLS, F32) for _ in range(2)]
        pT = [split(PCOLS) for _ in range(2)]
        x_sb = arena[:, taken[0]:taken[0] + NT * D]
        oT = split(2 * GH * S)
        before = arena[0:1, 0:R_TILES * E_ROUTED].rearrange("p (i e) -> p i e", e=E_ROUTED)
        taken[0] = 0
        xT = [split(KC * P) for _ in range(2)]
        xs = carve(4 * D, F32).rearrange("p (r d) -> p r d", r=4)
        ys = carve(4 * D, F32).rearrange("p (r d) -> p r d", r=4)
        sg = carve(2 * INTER, F32).rearrange("p (r n) -> p r n", r=2)
        hid = carve(4 * INTER, F32)
        hT = [w.rearrange("p (r n) -> p r n", r=4) for w in split(4 * 2 * P)]
        hT_flat = [w.rearrange("p r n -> p (r n)") for w in hT]
        AHEAD = 2
        assert 4 * taken[0] + AHEAD * 2 * WE <= 2 * 2 * (2 * KC * 512 + KC * 2048)
        expert_at = arena[:, taken[0]:]
        expert_s = split(E_ROUTED * WE)
        nmax = sb("nmax", [P, 2, QT], F32)
        waited = sb("waited", [P, 2, len(SCORE_UNITS)], F32)
        rsum = sb("rsum", [P, 2, QT], F32)
        rinv = sb("rinv", [P, 2, QT], F32)
        x_back = stage[:, 0:NT * D].rearrange("p (t d) -> p t d", d=D)
        back = expert_at[:, 0:NT * TOP_K * D].rearrange("p (t k d) -> p t k d", t=NT, k=TOP_K)

        xs_dram = nc.dram_tensor("xs_dram", (R_TILES * P, DX), F32).ap()
        ys_dram = nc.dram_tensor("ys_dram", ((TOP_K * NT + R_TILES) * P, D), F32).ap()

        bank = [ctx.enter_context(nc.psum_tensor(f"bank{n}", [P, 512], F32)) for n in range(8)]
        score_bank, pt_bank, o_bank, misc_bank = bank[0:3], bank[3:5], bank[5], bank[6:8]
        gu_bank, hT_bank, y_bank, xT_bank = bank[0:2], bank[2:4], bank[4:6], bank[6:8]
        xnT_bank = bank[6:8]

        x_in, ident_in, const_in, tab_in, gate_in = [sem("x_in0"), sem("x_in1"), sem("x_in2")], sem("ident_in"), sem("const_in"), sem("tab_in"), sem("gate_in")
        stage_in = [sem(f"stage_in{n}") for n in range(NSTG)]
        const_cast, zeroed, filled, fill_out, mask_zero = sem("const_cast"), sem("zeroed"), sem("filled"), sem("fill_out"), sem("mask_zero")
        w_hi, w_lo = sem("w_hi"), sem("w_lo")
        var_ready, rooted = sem("var_ready"), sem("rooted")
        gate_lo, scaled, xn_first, xn_ready, xnT_ps, xnT_hi, xnT_lo = sem("gate_lo"), sem("scaled"), sem("xn_first"), sem("xn_ready"), sem("xnT_ps"), sem("xnT_hi"), sem("xnT_lo")
        rt, rt_shift, rt_exp, rt_sum, picked, chosen = sem("rt"), sem("rt_shift"), sem("rt_exp"), sem("rt_sum"), sem("picked"), sem("chosen")
        slots_ready, tile_part, tiles_ready = sem("slots_ready"), sem("tile_part"), sem("tiles_ready")
        rows_ready, scattered, rows_known = sem("rows_ready"), sem("scattered"), sem("rows_known")
        meta_in = sem("meta_in")
        scores, maxed, exped, inverted, normed = sem("scores"), sem("maxed"), sem("exped"), sem("inverted"), sem("normed")
        pt_ps, pt_hi, pt_lo = sem("pt_ps"), sem("pt_hi"), sem("pt_lo")
        pv, o_hi, o_lo = sem("pv"), sem("o_hi"), sem("o_lo")
        misc_ps, misc_free = sem("misc_ps"), sem("misc_free")
        rot_add, rot_hi, rot_lo, v_hi = sem("rot_add"), sem("rot_hi"), sem("rot_lo"), sem("v_hi")
        shared_in, shared_hi, shared_w = sem("shared_in"), sem("shared_hi"), sem("shared_w")
        expert_in = [sem(f"expert_in{n}") for n in range(ERING)]
        expert_hi, even_lo, odd_lo = sem("expert_hi"), sem("even_lo"), sem("odd_lo")
        xs_in = [sem(f"xs_in{n}") for n in range(4)]
        ys_out = [sem(f"ys_out{n}") for n in range(4)]
        xT_ps, xT_hi, xT_lo, ys_ready = sem("xT_ps"), sem("xT_hi"), sem("xT_lo"), sem("ys_ready")
        gu_ps, silued, hidden, hT_ps, hT_hi, hT_lo, down_ps, y_done = (
            sem("gu_ps"), sem("silued"), sem("hidden"), sem("hT_ps"), sem("hT_hi"), sem("hT_lo"), sem("down_ps"), sem("y_done"))
        back_in = [sem(f"back_in{n}") for n in range(GROUPS)]
        x_again = sem("x_again")
        pair_sum, ffn_sum, gate_act, gated, summed, stored = sem("pair_sum"), sem("ffn_sum"), sem("gate_act"), sem("gated"), sem("summed"), sem("stored")

        PASSES = ((0, 0), (0, 1), (1, 0))

        W_CHUNKS = ["k", "q0", "v", "q1", "q2", "o0", "q3", "o1", "o2", "o3"]
        N_CHUNKS = len(W_CHUNKS)
        W_FIRST = 4

        def w_split(n):
            name = W_CHUNKS[n]
            dst = {"k": wkv_s, "v": wkv_s, "q": wq_s, "o": wo_s}[name[0]]
            at = {"k": 0, "v": 1}[name] if len(name) == 1 else int(name[1])
            return [t[:, at * SCOLS:(at + 1) * SCOLS] for t in dst]

        def w_stage(n):
            return stage[:, n % NSTG * SCOLS:(n % NSTG + 1) * SCOLS]

        X_TILES = (slice(0, QT), slice(QT, 2 * QT), slice(2 * QT, NT))
        LN_TILES = (slice(0, QT), slice(QT, NT))
        FILL_TILES = R_TILES // FILLS
        SCATTERED = 16 * TOP_K * NT
        fill = s_sb[:, 0:FILL_TILES * DX].rearrange("p (t d) -> p t d", d=DX)
        def o_cols(rd, j):
            return bass.ds(((rd.i + (j < 0)) % 2) * (GH * S) + j % GH * S, S)

        SHARED_AT = (ERING - E_SHARED) * WE

        def shared_parts(half):
            middle, full = SHARED_W // 2, SHARED_W - D
            parts = ((P, 0, middle),) if half == 0 else ((P, middle, full), (SHARED_ROWS[-1], full, SHARED_W))
            return [(slice(0, rows_), slice(a, b), slice(SHARED_AT + a, SHARED_AT + b)) for rows_, a, b in parts]

        def expert_lo(engine, e):
            at, st = e * WE, e % ERING * WE
            for rows_, a, b in ((slice(0, P), 0, WG), (slice(0, HC), WG, WE)):
                ins = engine.tensor_tensor(expert_s[1][rows_, at + a:at + b], stage[rows_, st + a:st + b],
                                           expert_s[0][rows_, at + a:at + b], ALU.subtract)
            return ins

        def hidden_parts(st):
            if st.routed(1):
                at = st.ring(4, 1) * 2 * P
                return [(slice(0, HC), slice(at, at + 2 * P), slice(0, 2 * P))]
            at, full = st.pair(1) * 2 * P, (len(SHARED_ROWS) - 1) * P
            return [(slice(0, P), slice(at, at + full), slice(0, full)),
                    (slice(0, SHARED_ROWS[-1]), slice(at + full, at + full + P), slice(full, full + P))]

        block = ctx.enter_context(nc.Block())

        @block.sync
        def _(sp):
            x_t, x_at = x.rearrange("b (t p) d -> p (b t) d", p=P), x_sb.rearrange("p (t d) -> p t d", d=D)

            def load_weights(n):
                name = W_CHUNKS[n]
                if name[0] == "o":
                    host = wo[int(name[1]) * GH * DH:(int(name[1]) + 1) * GH * DH, :].rearrange("(h p) n -> p h n", p=P)
                else:
                    host = {"k": wk, "v": wv, "q": wq}[name[0]].rearrange("(c p) n -> p c n", p=P)
                    if name[0] == "q":
                        host = host[:, :, int(name[1]) * GH * DH:(int(name[1]) + 1) * GH * DH]
                if n >= NSTG:
                    sp.wait_ge(w_lo, n - NSTG + 1)
                sp.dma_start(w_stage(n).rearrange("p (c n) -> p c n", n=host.shape[2]), host).then_inc(stage_in[n % NSTG], 16)

            def load_x(g):
                sp.dma_start(x_at[:, X_TILES[g]], x_t[:, X_TILES[g]]).then_inc(x_in[g], 16)

            load_x(0)
            sp.dma_start(ident_f[:], ident).then_inc(ident_in, 16)
            load_weights(0)
            load_weights(1)
            load_x(1)
            load_x(2)
            sp.dma_start(tab[:], rope.rearrange("a p s -> p a s")).then_inc(tab_in, 16)
            for n in range(2, W_FIRST):
                load_weights(n)
            for dst, host in ((mask_f, mask), (tri_f, tri), (iota_f[:], iota), (row_id[:], rows), (digit[:], digits)):
                sp.dma_start(dst, host).then_inc(const_in, 16)
            for n in range(W_FIRST, N_CHUNKS):
                load_weights(n)
            sp.wait_ge(filled, 1)
            xs_tiles = xs_dram.rearrange("(t p) d -> p t d", p=P)
            for c in range(FILLS):
                sp.dma_start(xs_tiles[:, c * FILL_TILES:(c + 1) * FILL_TILES], fill).then_inc(fill_out, 16)

            sp.wait_ge(w_lo, N_CHUNKS)
            for half in range(E_SHARED):
                for c in range(KC):
                    at = SHARED_AT + half * WG + c * GU
                    sp.dma_start(stage[:, at:at + GU].rearrange("p (w n) -> p w n", w=2),
                                 shared_gu[c * P:(c + 1) * P, :].rearrange("p (w n) -> p w n", w=2)[:, :, half * INTER:(half + 1) * INTER]
                                 ).then_inc(shared_in, 16)
            full, at = len(SHARED_ROWS) - 1, SHARED_AT + SHARED_WG
            sp.dma_start(stage[:, at:at + full * D].rearrange("p (c n) -> p c n", c=full),
                         shared_down[0:full * P, :].rearrange("(c p) n -> p c n", p=P)).then_inc(shared_in, 16)
            sp.dma_start(stage[0:SHARED_ROWS[-1], at + full * D:at + (full + 1) * D], shared_down[full * P:, :]).then_inc(shared_in, 16)

            for e in range(E_ROUTED):
                if e == ERING - E_SHARED:
                    sp.wait_ge(shared_w, 2)
                if e >= ERING:
                    sp.wait_ge(odd_lo if (e - ERING) % 2 else even_lo, (e - ERING) // 2 + 1)
                at = e % ERING * WE
                sp.dma_start(stage[:, at:at + WG].rearrange("p (c n) -> p c n", c=KC),
                             w_gate_up[e].rearrange("(c p) n -> p c n", p=P)).then_inc(expert_in[e % ERING], 16)
                sp.dma_start(stage[0:HC, at + WG:at + WE].rearrange("p (c n) -> p c n", c=2),
                             w_down[e].rearrange("(c p) n -> p c n", p=HC)).then_inc(expert_in[e % ERING], 16)
                if e == E_ROUTED - 1:
                    sp.wait_ge(scattered, SCATTERED)
                    sp.dma_start(meta[:], xs_tiles[:, :, D:DX]).then_inc(meta_in, 16)

            def load_rows(m, k):
                sp.dma_start(xs[:, k, :], xs_dram[bass.ds(m * P, P), 0:D]).then_inc(xs_in[k], 16)

            sp.wait_ge(tiles_ready, 1)
            for m in range(4):
                load_rows(m, m)
            with sp.Fori(1, R_TILES // 4) as r:
                for k in range(4):
                    sp.wait_ge(xT_ps, r * 4 + k - 3)
                    load_rows(r * 4 + k, k)

            sp.wait_ge(even_lo, E_ROUTED // 2)
            sp.wait_ge(odd_lo, E_ROUTED // 2)
            sp.dma_start(x_back, x_t).then_inc(x_again, 16)

            sp.wait_ge(down_ps, SH_TILES + R_TILES)
            for n in range(4):
                sp.wait_ge(ys_out[n], 16 * (R_TILES // 4))
            ys_t = ys_dram[0:TOP_K * TOK, :].rearrange("(t p k) d -> p t k d", p=P, k=TOP_K)
            for g in range(GROUPS):
                t = slice(g * BACK, (g + 1) * BACK)
                sp.dma_start(back[:, t], ys_t[:, t]).then_inc(back_in[g], 16)
            out_t = out.rearrange("b (t p) d -> p (b t) d", p=P)
            for g in range(GROUPS):
                sp.wait_ge(summed, g + 1)
                t = slice(g * BACK, (g + 1) * BACK)
                sp.dma_start(out_t[:, t], s_sb[:, t.start * D:t.stop * D].rearrange("p (t d) -> p t d", d=D)).then_inc(stored, 16)
            sp.wait_ge(stored, 16 * GROUPS)

        @block.gpsimd
        def _(pool):
            pool.memset(s_sb[:], 0.0).then_inc(zeroed, 1)
            pool.memset(one[:], 1.0).then_inc(zeroed, 1)
            pool.memset(ones_b[:], 1.0).then_inc(zeroed, 1)
            pool.memset(mask_b[:, 0:S - P], 0.0).then_inc(mask_zero, 1)
            def weights_lo(n):
                hi, lo = w_split(n)
                pool.wait_ge(w_hi, n + 1)
                pool.tensor_tensor(lo, w_stage(n), hi, ALU.subtract).then_inc(w_lo, 1)

            for n in range(W_FIRST - 1):
                weights_lo(n)

            def rotate_sum(name, item):
                buf = ROT_BUF[name]
                pool.wait_ge(misc_free, item)
                pool.tensor_tensor(rot_a[buf], rot_a[buf], rot_b[buf], ALU.add).then_inc(rot_add, 1)

            def rotate_lo(name, count, bufs=ROT_BUF):
                buf = bufs[name]
                dst = kT[1] if name == "k" else qT[1][:, int(name[1]) * S:(int(name[1]) + 1) * S]
                hi = kT[0] if name == "k" else qT[0][:, int(name[1]) * S:(int(name[1]) + 1) * S]
                pool.wait_ge(rot_hi, count)
                pool.tensor_tensor(dst, rot_a[buf], hi, ALU.subtract).then_inc(rot_lo, 1)

            def divide(h, par):
                pool.wait_ge(inverted, h + 1)
                for qt in range(QT):
                    pr = probs[par][:, P_AT[qt]:P_AT[qt] + (qt + 1) * P]
                    ins = pool.tensor_tensor(pr, pr, rinv[:, par, qt:qt + 1].to_broadcast([P, (qt + 1) * P]), ALU.mult)
                ins.then_inc(normed, 1)

            rotate_lo("q0", PROLOGUE.rot("q0"))
            rotate_lo("k", PROLOGUE.rot("k"))
            rotate_sum("q1", PROLOGUE.item("q1"))
            rotate_lo("q1", PROLOGUE.rot("q1"))
            divide(0, 0)
            rotate_lo("q2", PROLOGUE.rot("q2"), ROT_BUF_PROLOGUE)
            pool.wait_ge(const_in, 16 * 5)
            pool.wait_ge(zeroed, 1)
            pool.tensor_copy(fill[:, :, D + 1], row_id[:, TOP_K * NT:TOP_K * NT + FILL_TILES]).then_inc(filled, 1)

            def scatter():
                for n in range(TOP_K):
                    pool.indirect_dma_start(xs_dram, bass.IndirectOffsetOnAxis(slot_now[:, n:n + 1], 0),
                                            rows_out[:, n, :], None).then_inc(scattered, 16)

            def round_(rd):
                for j in range(GH - 1):
                    if j == 0:
                        rotate_sum("q3", rd.base)
                    elif not rd.last:
                        rotate_sum(f"q{j - 1}", rd.item(f"q{j - 1}"))
                    if j == 1 and rd.tile() is not None:
                        pool.wait_ge(rows_ready, rd.tile() + 1)
                    divide(rd.head(j + 1), (j + 1) % 2)
                    if j == 2 and not rd.last:
                        rotate_sum("k", rd.item("k"))
                    if j == 0:
                        rotate_lo("q3", rd.i * 5 + 5)
                    elif not rd.last:
                        rotate_lo(f"q{j - 1}", rd.rot(f"q{j - 1}"))
                    if rd.early and j < 2:
                        weights_lo(W_FIRST + 2 * rd.i + j)
                    if j == 1 and rd.tile() is not None:
                        scatter()
                if not rd.last:
                    rotate_lo("k", rd.rot("k"))
                    rotate_sum("q2", rd.item("q2"))
                    divide(rd.head(GH), 0)
                    rotate_lo("q2", rd.rot("q2"))
                    if rd.first:
                        pool.wait_ge(fill_out, 16 * FILLS)
                        pool.memset(fill[:, :, D + 1], 0.0).then_inc(zeroed, 1)

            def scatter_tile(t):
                pool.wait_ge(rows_ready, t + 1)
                scatter()

            round_(Round(0, "first"))
            round_(Round(1, "second"))
            round_(Round(2, "third"))
            scatter_tile(0)
            with pool.Fori(3, NG - 1) as i:
                round_(Round(i, "loop"))
            round_(Round(NG - 1, "last"))
            scatter_tile(NT - 2)
            scatter_tile(NT - 1)

            for e in range(0, E_ROUTED, 2):
                pool.wait_ge(expert_hi, e + 1)
                expert_lo(pool, e).then_inc(even_lo, 1)

            pool.wait_ge(rows_known, 1)
            for m in range(R_TILES):
                pool.wait_ge(ys_ready, m + 1)
                pool.indirect_dma_start(ys_dram, bass.IndirectOffsetOnAxis(row_u[:, m:m + 1], 0),
                                        ys[:, m % 4, :], None).then_inc(ys_out[m % 4], 16)

            for g in range(GROUPS):
                t = slice(g * BACK, (g + 1) * BACK)
                y = y_sb[:, t.start * D:t.stop * D].rearrange("p (t d) -> p t d", d=D)
                pool.wait_ge(back_in[g], 16)
                pool.tensor_tensor(back[:, t, 0, :], back[:, t, 0, :], back[:, t, 1, :], ALU.add).then_inc(pair_sum, 1)
                pool.wait_ge(y_done, (g + 1) * BACK)
                pool.wait_ge(pair_sum, g + 1)
                pool.tensor_tensor(y, y, back[:, t, 0, :], ALU.add).then_inc(ffn_sum, 1)

        @block.scalar
        def _(act):
            act.dma_start(gate_f[:], gate_t.rearrange("(c p) e -> p c e", p=P)).then_inc(gate_in, 16)
            act.wait_ge(gate_in, 16)
            act.copy(gate_s[0][:], gate_f[:].rearrange("p c e -> p (c e)")).then_inc(const_cast, 1)
            def root_of(g):
                act.wait_ge(var_ready, g + 1)
                act.activation(root[:, LN_TILES[g]], var[:, LN_TILES[g]], ACT.Sqrt).then_inc(rooted, 1)

            def weights_hi(n):
                act.wait_ge(stage_in[n % NSTG], 16 * (n // NSTG + 1))
                act.copy(w_split(n)[0], w_stage(n)).then_inc(w_hi, 1)

            def normalise(b):
                act.wait_ge(scaled, 1)
                for t in range(b * QT, (b + 1) * QT):
                    ins = act.activation(xn_t[:, t, :], x_sb[:, t * D:(t + 1) * D], ACT.Identity,
                                         scale=rstd[:, t:t + 1], bias=shift[:, t:t + 1])
                ins.then_inc(xn_ready, 1)

            def xnT_hi_part(b, c, ps):
                act.copy(xnT[0][:, c * TOK + b * S:c * TOK + (b + 1) * S], ps).then_inc(xnT_hi, 1)

            def x_item_hi(rd, name):
                act.wait_ge(misc_ps, rd.item(name))
                xnT_hi_part(int(name[1]), int(name[2]), misc_bank[rd.bank(name)][:])

            root_of(0)
            weights_hi(0)
            weights_hi(1)
            for c in range(KC):
                act.wait_ge(xnT_ps, c + 1)
                xnT_hi_part(0, c, xnT_bank[c][:])
            root_of(1)
            act.wait_ge(ident_in, 16)
            act.copy(ident_b[:], ident_f[:]).then_inc(const_cast, 1)
            weights_hi(2)
            weights_hi(3)

            def rotate_hi(name, count, bufs=ROT_BUF):
                act.wait_ge(rot_add, count)
                dst = kT[0] if name == "k" else qT[0][:, int(name[1]) * S:(int(name[1]) + 1) * S]
                act.copy(dst, rot_a[bufs[name]]).then_inc(rot_hi, 1)

            def value_hi(rd):
                act.wait_ge(misc_ps, rd.item("v"))
                act.copy(v_s[0], misc_bank[rd.bank("v")][:]).then_inc(v_hi, 1)

            def exponentials(h, par, units=(0, 1, 2)):
                for u in units:
                    unit = SCORE_UNITS[u]
                    act.wait_ge(maxed, h * 3 + u + 1)
                    for qt, col in unit:
                        n = (qt + 1) * P
                        ins = act.activation(probs[par][:, P_AT[qt]:P_AT[qt] + n], score_bank[u][:, col:col + n], ACT.Exp, scale=-1.0,
                                             bias=nmax[:, par, qt:qt + 1], accum_out=rsum[:, par, qt:qt + 1])
                    ins.then_inc(exped, 1)

            def probs_hi(h, j, units):
                for u in units:
                    at, cols = PT_UNIT_COLS[u]
                    act.wait_ge(pt_ps, h * 3 + u + 1)
                    act.copy(pT[j % 2][0][:, at:at + cols], pt_bank[(3 * j + u) % 2][:, 0:cols]).then_inc(pt_hi, 1)

            def set_out(t):
                act.wait_ge(slots_ready, 1)
                if not isinstance(t, int) or t > 0:
                    act.wait_ge(scattered, t * (16 * TOP_K))
                for n in range(TOP_K):
                    act.copy(rows_out[:, n, 0:D], xn[:, bass.ds(t * D, D)])
                act.copy(rows_out[:, :, D:DX], tags[:, bass.ds(t, 1)].rearrange("p o n w -> p (o n) w"))
                act.copy(slot_now[:], slot_to[:, bass.ds(t, 1)].rearrange("p o n -> p (o n)")).then_inc(rows_ready, 1)

            def output_hi(rd, j):
                act.wait_ge(pv, rd.head(j) + 1)
                act.copy(oT[0][:, o_cols(rd, j)], o_bank[:]).then_inc(o_hi, 1)

            rotate_hi("q0", PROLOGUE.rot("q0"))
            act.wait_ge(const_in, 16 * 5)
            act.copy(mask_b[:, S - P:S], mask_f).then_inc(const_cast, 1)
            act.copy(tri_b[:], tri_f).then_inc(const_cast, 1)
            rotate_hi("k", PROLOGUE.rot("k"))
            exponentials(0, 0, (0,))
            rotate_hi("q1", PROLOGUE.rot("q1"))
            exponentials(0, 0, (1, 2))
            normalise(1)
            rotate_hi("q2", PROLOGUE.rot("q2"), ROT_BUF_PROLOGUE)
            normalise(2)

            def x_items_hi(rd, items):
                for name in items:
                    x_item_hi(rd, name)

            def shared_hi_part(half):
                act.wait_ge(shared_in, 16 * (KC * E_SHARED + 2))
                for rows_, to, at in shared_parts(half):
                    ins = act.copy(shared_s[0][rows_, to], stage[rows_, at])
                ins.then_inc(shared_hi, 1)

            def round_(rd):
                for j in range(GH - 1):
                    h, par = rd.head(j + 1), (j + 1) % 2
                    if rd.second and j == 1:
                        act.wait_ge(rt_shift, 1)
                        act.activation(prob[:], prob[:], ACT.Exp).then_inc(rt_exp, 1)
                    if j == 2:
                        output_hi(rd, 0)
                    if j == 0:
                        if rd.first:
                            probs_hi(rd.head(j), j, (0, 1))
                        exponentials(h, par)
                        if not rd.first:
                            probs_hi(rd.head(j), j, (0, 1))
                        rotate_hi("q3", rd.i * 5 + 5)
                        if not rd.first:
                            output_hi(rd, -1)
                        value_hi(rd)
                        probs_hi(rd.head(j), j, (2,))
                        if rd.tile() is not None:
                            set_out(rd.tile())
                    else:
                        probs_hi(rd.head(j), j, (0, 1))
                        exponentials(h, par)
                        if rd.first:
                            x_items_hi(rd, X_BEFORE[j])
                        if not rd.last:
                            rotate_hi(f"q{j - 1}", rd.rot(f"q{j - 1}"))
                        probs_hi(rd.head(j), j, (2,))
                    if rd.first:
                        x_items_hi(rd, X_AFTER[j])
                        if j == 0:
                            normalise(3)
                    if rd.early and j < 2:
                        weights_hi(W_FIRST + 2 * rd.i + j)
                    if rd.last and j > 0:
                        shared_hi_part(j - 1)
                output_hi(rd, 1)
                if rd.first:
                    x_items_hi(rd, X_AFTER[GH - 1])
                if not rd.last:
                    rotate_hi("k", rd.rot("k"))
                probs_hi(rd.head(3), 3, (0, 1))
                output_hi(rd, 2)
                if rd.last:
                    set_out(NT - 2)
                else:
                    exponentials(rd.head(GH), 0)
                    rotate_hi("q2", rd.rot("q2"))
                probs_hi(rd.head(3), 3, (2,))

            round_(Round(0, "first"))
            round_(Round(1, "second"))
            round_(Round(2, "third"))
            set_out(0)
            with act.Fori(3, NG - 1) as i:
                round_(Round(i, "loop"))
            round_(Round(NG - 1, "last"))
            output_hi(EPILOGUE, -1)

            def expert_hi_part(e):
                act.wait_ge(expert_in[e % ERING], 32 * (e // ERING + 1))
                if e == AHEAD:
                    act.wait_ge(misc_free, ATTENTION_ITEMS)
                at, st = e * WE, e % ERING * WE
                act.copy(expert_s[0][:, at:at + WG], stage[:, st:st + WG])
                act.copy(expert_s[0][0:HC, at + WG:at + WE], stage[0:HC, st + WG:st + WE]).then_inc(expert_hi, 1)

            for e in range(AHEAD):
                expert_hi_part(e)
            set_out(NT - 1)

            def step(st):
                n = st.n
                if st.gu:
                    act.wait_ge(gu_ps, n + 1)
                    act.activation(sg[:, st.ring(2), :], gu_bank[st.ring(2)][:, 0:INTER], ACT.Silu).then_inc(silued, 1)
                if st.t:
                    act.wait_ge(hT_ps, st.layers(1))
                    for rows_, to, at in hidden_parts(st):
                        ins = act.copy(hT_flat[0][rows_, to], hT_bank[st.parity(1)][rows_, at])
                    ins.then_inc(hT_hi, 1)
                if st.rows:
                    act.wait_ge(xT_ps, st.tile(-2) + 1)
                    act.copy(xT[st.ring(2)][0], xT_bank[st.ring(2)][:, 0:KC * P]).then_inc(xT_hi, 1)
                if st.y and st.routed(LAG):
                    m = st.tile(LAG)
                    act.wait_ge(down_ps, st.layers(LAG))
                    if st.like - LAG - SH_FIRST >= 4:
                        act.wait_ge(ys_out[st.ring(4, LAG)], stored_rows(st))
                    act.activation(ys[:, st.ring(4, LAG), :], y_bank[st.parity(LAG)][:, 0:D], ACT.Copy,
                                   scale=meta[:, bass.ds(m, 1), 0]).then_inc(ys_ready, 1)
                if st.like == SH_FIRST - 2:
                    act.wait_ge(meta_in, 16)
                    act.copy(row_u[:], meta[:, :, 1]).then_inc(rows_known, 1)
                if st.out is not None:
                    gate(st.out)
                if st.like < E_ROUTED - AHEAD:
                    expert_hi_part(st.like + AHEAD)

            def gate(g):
                act.wait_ge(ffn_sum, g + 1)
                cols = slice(g * BACK * D, (g + 1) * BACK * D)
                act.activation(y_sb[:, cols], y_sb[:, cols], ACT.Silu).then_inc(gate_act, 1)

            def stored_rows(st):
                m = st.tile(LAG)
                return (m - st.ring(4, LAG)) * 4

            ffn_steps(act, step)
            for g in range(EARLY, GROUPS):
                gate(g)

        @block.vector
        def _(dve):
            chain = [0]

            def then(ins):
                chain[0] += 1
                ins.then_inc(rt, 1)
                dve.wait_ge(rt, chain[0])

            dve.wait_ge(const_cast, 1)
            dve.tensor_tensor(gate_s[1][:], gate_f[:].rearrange("p c e -> p (c e)"), gate_s[0][:], ALU.subtract).then_inc(gate_lo, 1)

            def statistics(g):
                dve.wait_ge(x_in[g], 16)
                for t in range(NT)[X_TILES[g]]:
                    ins = dve.bn_stats(stats[:, t, :], x_sb[:, t * D:(t + 1) * D])
                then(ins)

            def variances(g):
                for t in range(NT)[LN_TILES[g]]:
                    ins = dve.bn_aggr(mv[:, t, :], stats[:, t, :])
                then(ins)
                dve.tensor_scalar(var[:, LN_TILES[g]], mv[:, LN_TILES[g], 1], EPS, None, ALU.add).then_inc(var_ready, 1)

            def invert_roots(g):
                t = LN_TILES[g]
                v, r, inv = var[:, t], root[:, t], rstd[:, t]
                dve.wait_ge(rooted, g + 1)
                then(dve.reciprocal(inv, r))
                then(dve.tensor_tensor(r, inv, inv, ALU.mult))
                then(dve.tensor_tensor(r, r, v, ALU.mult))
                then(dve.tensor_scalar(r, r, -0.5, 1.5, ALU.mult, ALU.add))
                then(dve.tensor_tensor(inv, inv, r, ALU.mult))

            def normalise_first():
                for t in range(QT):
                    dve.tensor_scalar(xn_t[:, t, :], x_sb[:, t * D:(t + 1) * D], mv[:, t, 0:1], rstd[:, t:t + 1],
                                      ALU.subtract, ALU.mult).then_inc(xn_first, 1)

            def shifts():
                t = LN_TILES[1]
                then(dve.tensor_tensor(shift[:, t], mv[:, t, 0], rstd[:, t], ALU.mult))
                dve.tensor_scalar(shift[:, t], shift[:, t], -1.0, None, ALU.mult).then_inc(scaled, 1)

            def xnT_lo_part(b, c, ps):
                at = c * TOK + b * S
                dve.wait_ge(xnT_hi, b * KC + c + 1)
                return dve.tensor_tensor(xnT[1][:, at:at + S], ps, xnT[0][:, at:at + S], ALU.subtract)

            def x_items_lo(rd, items):
                for name in items:
                    xnT_lo_part(int(name[1]), int(name[2]), misc_bank[rd.bank(name)][:]).then_inc(misc_free, 1)

            statistics(0)
            variances(0)
            invert_roots(0)
            normalise_first()
            statistics(1)
            for c in range(KC):
                xnT_lo_part(0, c, xnT_bank[c][:]).then_inc(xnT_lo, 1)
            statistics(2)
            variances(1)

            TE = [P, NT, E_ROUTED]

            def over_e(ap):
                return ap.rearrange("p (t o) -> p t o", o=1).to_broadcast(TE)

            def over_t(ap):
                return ap.rearrange("p (o e) -> p o e", o=1).to_broadcast(TE)

            def route(part):
                if part == 0:
                    for t in range(NT):
                        ins = dve.max(top[:, t, :], logit[:, t, :])
                    then(ins)
                    dve.tensor_tensor(prob[:], logit[:], top[:, :, 0:1].to_broadcast(TE), ALU.subtract).then_inc(rt_shift, 1)
                if part == 1:
                    for t in range(NT):
                        ins = dve.max_index(topi[:, t, :], top[:, t, :], logit[:, t, :])
                    then(ins)
                    dve.tensor_copy(topf[:], topi[:, :, 0:2]).then_inc(picked, 1)
                if part == 2:
                    dve.wait_ge(picked, 1)
                    for n in range(TOP_K):
                        ins = dve.tensor_tensor(sel[n][:], over_t(iota_f[:, 0:E_ROUTED]), topf[:, :, n:n + 1].to_broadcast(TE), ALU.is_equal)
                    then(ins)
                    dve.tensor_tensor(sel_b[:].rearrange("p (t e) -> p t e", e=E_ROUTED), sel[0][:], sel[1][:], ALU.add).then_inc(chosen, 1)
                if part == 3:
                    dve.wait_ge(rt_exp, 1)
                    for n in range(TOP_K):
                        dve.tensor_tensor(pick[n][:], sel[n][:], prob[:], ALU.mult)
                    then(dve.tensor_reduce(zsum[:], prob[:], AX.X, ALU.add))
                    dve.reciprocal(zsum[:], zsum[:]).then_inc(rt_sum, 1)
                if part == 4:
                    dve.wait_ge(rt_sum, 1)
                    for n in range(TOP_K):
                        then(dve.tensor_reduce(weight[:], pick[n][:], AX.X, ALU.add))
                        then(dve.tensor_tensor(tags[:, :, n, 0], weight[:], zsum[:], ALU.mult))
                        dve.tensor_copy(tags[:, :, n, 1], row_id[:, n * NT:(n + 1) * NT])

            def place(rd, part):
                if part == 0:
                    rank_bank = misc_bank[rd.bank("rank")]
                    dve.wait_ge(misc_ps, rd.item("rank"))
                    ranks = rank_bank[:, 0:NT * E_ROUTED].rearrange("p (t e) -> p t e", e=E_ROUTED)
                    counts = rank_bank[:, NT * E_ROUTED:2 * NT * E_ROUTED].rearrange("p (t e) -> p e t", e=E_ROUTED)
                    then(dve.tensor_copy(count, counts))
                    flat = count.rearrange("p e t -> p (e t)")
                    then(dve.tensor_tensor_scan(total[:].rearrange("p e t -> p (e t)"), flat, flat, 0.0, ALU.add, ALU.max))
                    then(dve.tensor_tensor(count, total[:], count, ALU.subtract))
                    dve.tensor_tensor(slot[:], ranks, count.rearrange("p e t -> p t e"), ALU.add).then_inc(misc_free, 1)
                if part == 1:
                    dve.wait_ge(misc_free, rd.base)
                    dve.memset(ends[:, 0:1], 0.0)
                    dve.tensor_scalar(steps128[:], iota_f[:, 0:E_ROUTED], float(P), None, ALU.mult)
                    then(dve.tensor_copy(ends[:, 1:E_ROUTED + 1], total[:, :, NT - 1]))
                    then(dve.tensor_tensor(held[:], ends[:, 1:E_ROUTED + 1], ends[:, 0:E_ROUTED], ALU.subtract))
                    EM = [P, E_ROUTED, E_ROUTED]
                    over = compare[:, 0:E_ROUTED * E_ROUTED].rearrange("p (e m) -> p e m", m=E_ROUTED)
                    then(dve.tensor_tensor(over, held[:].rearrange("p (e o) -> p e o", o=1).to_broadcast(EM),
                                           steps128[:].rearrange("p (o m) -> p o m", o=1).to_broadcast(EM), ALU.is_gt))
                    then(dve.tensor_reduce(tiles[:], over, AX.X, ALU.add))
                    then(dve.tensor_tensor_scan(tiles_to[:], tiles[:], tiles[:], 0.0, ALU.add, ALU.max))
                    then(dve.tensor_tensor(offset[:], tiles_to[:], tiles[:], ALU.subtract))
                if part == 2:
                    then(dve.scalar_tensor_tensor(out=offset[:], in0=offset[:], scalar=float(P), in1=ends[:, 0:E_ROUTED],
                                                  op0=ALU.mult, op1=ALU.subtract))
                    then(dve.tensor_tensor(slot[:], slot[:], over_t(offset[:]), ALU.add))
                    for n in range(TOP_K):
                        ins = dve.tensor_tensor(pick[n][:], sel[n][:], slot[:], ALU.mult)
                    then(ins)
                    for n in range(TOP_K):
                        ins = dve.tensor_reduce(slot_to[:, :, n], pick[n][:], AX.X, ALU.add)
                    ins.then_inc(slots_ready, 1)

            def tile_experts(part):
                IE = [1, R_TILES, E_ROUTED]
                if part == 0:
                    dve.tensor_tensor(before, tiles_to[0:1, :].rearrange("p (o e) -> p o e", o=1).to_broadcast(IE),
                                      iota_f[0:1, :].rearrange("p (i o) -> p i o", o=1).to_broadcast(IE), ALU.is_le).then_inc(tile_part, 1)
                if part == 1:
                    dve.wait_ge(tile_part, 1)
                    dve.tensor_reduce(tile_e[:], before, AX.X, ALU.add).then_inc(tile_part, 1)
                if part == 2:
                    dve.wait_ge(tile_part, 2)
                    then(dve.tensor_scalar(tile_e[:], tile_e[:], float(E_ROUTED - 1), None, ALU.min))
                    then(dve.tensor_tensor(tile_e[:], tile_e[:], digit[:], ALU.mult))
                    in_group = tile_e[:].rearrange("p (i k) -> p i k", k=GROUP)
                    then(dve.tensor_reduce(group_e[:], in_group, AX.X, ALU.add))
                    for k in range(GROUP - LAG, GROUP):
                        then(dve.scalar_tensor_tensor(out=group_e[:, 1:], in0=in_group[:, :-1, k], scalar=float(E_ROUTED) ** -GROUP,
                                                      in1=group_e[:, 1:], op0=ALU.mult, op1=ALU.add))
                    dve.tensor_copy(group_u[:], group_e[:]).then_inc(tiles_ready, 1)

            def rotate_products(name, item, bank_n, freed, inverted_head=None, bufs=ROT_BUF):
                ps, buf = misc_bank[bank_n], bufs[name]
                cos, sin = (2, 3) if name == "k" else (0, 1)
                dve.wait_ge(misc_ps, item)
                if freed is not None:
                    dve.wait_ge(rot_lo, freed)
                dve.tensor_tensor(rot_a[buf], ps[:], tab[:, cos, :], ALU.mult)
                half = DH // 2
                if inverted_head is not None:
                    invert_sums(*inverted_head)
                dve.tensor_tensor(rot_b[buf][0:half, :], ps[half:DH, :], tab[half:DH, sin, :], ALU.mult)
                dve.tensor_tensor(rot_b[buf][half:DH, :], ps[0:half, :], tab[0:half, sin, :], ALU.mult).then_inc(misc_free, 1)

            def value_lo(rd):
                dve.wait_ge(v_hi, rd.i + 1)
                dve.tensor_tensor(v_s[1], misc_bank[rd.bank("v")][:], v_s[0], ALU.subtract).then_inc(misc_free, 1)

            def row_max(h, par, units=(0, 1, 2)):
                for u in units:
                    unit = SCORE_UNITS[u]
                    dve.wait_ge(scores, h * 3 + u + 1)
                    dve.tensor_tensor(waited[:, par, u:u + 1], one[:], one[:], ALU.mult)
                    for qt, col in unit:
                        n = (qt + 1) * P
                        ins = dve.tensor_tensor_reduce(score_bank[u][:, col:col + n], score_bank[u][:, col:col + n], mask_b[:, S - n:S],
                                                       -1.0, 3e38, ALU.add, ALU.min, nmax[:, par, qt:qt + 1])
                    ins.then_inc(maxed, 1)

            def invert_sums(h, par):
                dve.wait_ge(exped, h * 3 + 3)
                dve.reciprocal(rinv[:, par, :], rsum[:, par, :]).then_inc(inverted, 1)

            def probs_lo(h, j, units):
                for u in units:
                    at, cols = PT_UNIT_COLS[u]
                    dve.wait_ge(pt_hi, h * 3 + u + 1)
                    dve.tensor_tensor(pT[j % 2][1][:, at:at + cols], pt_bank[(3 * j + u) % 2][:, 0:cols], pT[j % 2][0][:, at:at + cols],
                                      ALU.subtract).then_inc(pt_lo, 1)

            def output_lo(rd, j):
                dve.wait_ge(o_hi, rd.head(j) + 1)
                cols = o_cols(rd, j)
                dve.tensor_tensor(oT[1][:, cols], o_bank[:], oT[0][:, cols], ALU.subtract).then_inc(o_lo, 1)

            def add_projection(rd, q):
                at = ((rd.i - 1) // NKV) * (QT * D) + q * D
                dve.wait_ge(misc_ps, rd.item(f"o{q}"))
                dve.wait_ge(misc_free, rd.item(f"o{q}") - 4)
                dve.tensor_tensor(s_sb[:, bass.ds(at, D)], misc_bank[rd.bank(f"o{q}")][:, 0:D], s_sb[:, bass.ds(at, D)],
                                  ALU.add).then_inc(misc_free, 1)

            def first_rope(name, freed=None, inverted_head=None):
                rotate_products(name, PROLOGUE.item(name), PROLOGUE.bank(name), freed, inverted_head, ROT_BUF_PROLOGUE)

            dve.wait_ge(tab_in, 16)
            def first_sum(name):
                buf = ROT_BUF_PROLOGUE[name]
                dve.wait_ge(misc_free, PROLOGUE.item(name))
                dve.tensor_tensor(rot_a[buf], rot_a[buf], rot_b[buf], ALU.add).then_inc(rot_add, 1)

            for name in ("q0", "k"):
                first_rope(name)
                first_sum(name)
            first_rope("q1")
            hi, lo = w_split(W_FIRST - 1)
            dve.wait_ge(w_hi, W_FIRST)
            dve.wait_ge(w_lo, W_FIRST - 1)
            dve.tensor_tensor(lo, w_stage(W_FIRST - 1), hi, ALU.subtract).then_inc(w_lo, 1)
            dve.wait_ge(const_cast, 4)
            dve.wait_ge(mask_zero, 1)
            dve.wait_ge(zeroed, 2)
            row_max(0, 0)
            invert_roots(1)
            shifts()
            first_rope("q2", PROLOGUE.rot("k"), (0, 0))
            first_sum("q2")

            def logits(rd):
                item = rd.item("logit")
                dve.wait_ge(misc_ps, item)
                dve.tensor_copy(logit[:], misc_bank[rd.bank("logit")][:, 0:NT * E_ROUTED].rearrange("p (t e) -> p t e", e=E_ROUTED)).then_inc(misc_free, 1)
                dve.wait_ge(const_in, 16 * 5)
                dve.wait_ge(misc_free, item)

            def shared_lo(half):
                dve.wait_ge(shared_hi, half + 1)
                for rows_, to, at in shared_parts(half):
                    ins = dve.tensor_tensor(shared_s[1][rows_, to], stage[rows_, at], shared_s[0][rows_, to], ALU.subtract)
                ins.then_inc(shared_w, 1)

            def round_(rd):
                i = rd.i
                freed = {"q0": i * 5 + 4, "q1": i * 5 + 5, "k": i * 5 + 3, "q2": i * 5 + 6, "q3": i * 5 + 7}
                if rd.first:
                    freed["q0"], freed["k"] = PROLOGUE.rot("q0"), PROLOGUE.rot("q2")

                def rope(name, inverted_head=None):
                    if not rd.last:
                        rotate_products(name, rd.item(name), rd.bank(name), freed[name], inverted_head)
                    elif inverted_head is not None:
                        invert_sums(*inverted_head)

                for j in range(GH - 1):
                    h, par = rd.head(j + 1), (j + 1) % 2
                    if j == 2:
                        output_lo(rd, 0)
                    row_max(h, par)
                    if j == 0:
                        if rd.first:
                            first_rope("q3", PROLOGUE.rot("q1"))
                            probs_lo(rd.head(j), j, (0, 1))
                        rope("q0", (h, par))
                        if not rd.first:
                            probs_lo(rd.head(j), j, (0, 1))
                        if not rd.first:
                            output_lo(rd, -1)
                        value_lo(rd)
                    else:
                        probs_lo(rd.head(j), j, (0, 1))
                        if rd.first:
                            x_items_lo(rd, X_BEFORE[j])
                        rope(("q0", "q1", "k")[j], (h, par))
                        if not rd.first:
                            add_projection(rd, j - 1)
                    probs_lo(rd.head(j), j, (2,))
                    if rd.first:
                        x_items_lo(rd, X_AFTER[j])
                    if rd.second:
                        if j < 2:
                            route(j + 1)
                        else:
                            place(rd, 0)
                    if rd.third:
                        if j == 0:
                            route(4)
                        else:
                            place(rd, j)
                output_lo(rd, 1)
                rope("q2")
                if rd.first:
                    x_items_lo(rd, X_AFTER[GH - 1])
                else:
                    add_projection(rd, 2)
                if rd.last:
                    shared_lo(0)
                probs_lo(rd.head(3), 3, (0, 1))
                if not rd.last:
                    row_max(rd.head(GH), 0)
                output_lo(rd, 2)
                if rd.last:
                    shared_lo(1)
                rope("q3", None if rd.last else (rd.head(GH), 0))
                probs_lo(rd.head(3), 3, (2,))
                if rd.first:
                    logits(rd)
                    route(0)
                else:
                    add_projection(rd, 3)
                if rd.second:
                    route(3)

            round_(Round(0, "first"))
            dve.wait_ge(zeroed, 4)
            round_(Round(1, "second"))
            round_(Round(2, "third"))
            with dve.Fori(3, NG - 1) as i:
                round_(Round(i, "loop"))
            round_(Round(NG - 1, "last"))
            output_lo(EPILOGUE, -1)
            for q in range(QT):
                add_projection(EPILOGUE, q)

            def finish(g):
                cols = slice(g * BACK * D, (g + 1) * BACK * D)
                if g == 0:
                    dve.wait_ge(misc_free, ATTENTION_ITEMS)
                    dve.wait_ge(x_again, 16)
                dve.wait_ge(gate_act, g + 1)
                dve.tensor_tensor(s_sb[:, cols], s_sb[:, cols], y_sb[:, cols], ALU.mult).then_inc(gated, 1)
                dve.wait_ge(gated, g + 1)
                s = s_sb[:, cols].rearrange("p (t d) -> p t d", d=D)
                dve.tensor_tensor(s, s, x_back[:, g * BACK:(g + 1) * BACK, :], ALU.add).then_inc(summed, 1)

            def step(st):
                n = st.n
                if st.gu:
                    dve.wait_ge(silued, n + 1)
                    dve.tensor_tensor(hid[:, st.ring(4) * INTER:(st.ring(4) + 1) * INTER], gu_bank[st.ring(2)][:, INTER:GU], sg[:, st.ring(2), :], ALU.mult).then_inc(hidden, 1)
                if st.t:
                    dve.wait_ge(hT_hi, st.layers(1))
                    for rows_, to, at in hidden_parts(st):
                        ins = dve.tensor_tensor(hT_flat[1][rows_, to], hT_bank[st.parity(1)][rows_, at], hT_flat[0][rows_, to], ALU.subtract)
                    ins.then_inc(hT_lo, 1)
                if st.rows:
                    dve.wait_ge(xT_hi, st.tile(-2) + 1)
                    dve.tensor_tensor(xT[st.ring(2)][1], xT_bank[st.ring(2)][:, 0:KC * P], xT[st.ring(2)][0], ALU.subtract).then_inc(xT_lo, 1)
                if st.y and not st.routed(LAG):
                    d = st.tile(LAG)
                    if d == 0:
                        dve.wait_ge(scattered, SCATTERED)
                    dve.wait_ge(down_ps, st.layers(LAG))
                    dve.tensor_copy(y_sb[:, d * D:(d + 1) * D], y_bank[st.parity(LAG)][:, 0:D]).then_inc(y_done, 1)
                if st.like in (3, 5, 7):
                    tile_experts((st.like - 3) // 2)
                odd = st.like + AHEAD - 1
                if odd < E_ROUTED and odd % 2:
                    dve.wait_ge(expert_hi, odd + 1)
                    expert_lo(dve, odd).then_inc(odd_lo, 1)
                if st.out is not None:
                    finish(st.out)

            ffn_steps(dve, step)
            for g in range(EARLY, GROUPS):
                finish(g)

        @block.tensor
        def _(pe):
            def transpose_xn(b, c, ps):
                for q in range(QT):
                    ins = pe.transpose(ps[:, q * P:(q + 1) * P], xn_t[:, b * QT + q, c * P:(c + 1) * P], ident_f[:])
                return ins

            def transpose_x_items(rd, items):
                for name in items:
                    b, c = int(name[1]), int(name[2])
                    pe.wait_ge(xn_ready, b)
                    pe.wait_ge(misc_free, rd.item(name) - 2)
                    transpose_xn(b, c, misc_bank[rd.bank(name)]).then_inc(misc_ps, 1)

            pe.wait_ge(ident_in, 16)
            for q in range(QT):
                pe.wait_ge(xn_first, q + 1)
                for c in range(KC):
                    ins = pe.transpose(xnT_bank[c][:, q * P:(q + 1) * P], xn_t[:, q, c * P:(c + 1) * P], ident_f[:])
                    if q == QT - 1:
                        ins.then_inc(xnT_ps, 1)

            def router(rd):
                pe.wait_ge(gate_lo, 1)
                pe.wait_ge(misc_free, rd.item("logit") - 2)
                ps = misc_bank[rd.bank("logit")]
                for t in range(NT):
                    for c in range(KC):
                        for n, (a, m) in enumerate(PASSES):
                            ins = pe.matmul(ps[:, t * E_ROUTED:(t + 1) * E_ROUTED], xnT[a][:, c * TOK + t * P:c * TOK + (t + 1) * P],
                                            gate_s[m][:, c * E_ROUTED:(c + 1) * E_ROUTED],
                                            start=(c == 0 and n == 0), stop=(c == KC - 1 and n == 2))
                ins.then_inc(misc_ps, 1)

            def rank(rd):
                pe.wait_ge(chosen, 1)
                pe.wait_ge(zeroed, 3)
                pe.wait_ge(misc_free, rd.item("rank") - 2)
                ps, n = misc_bank[rd.bank("rank")], NT * E_ROUTED
                pe.matmul(ps[:, 0:n], tri_b[:], sel_b[:], start=True, stop=True)
                pe.matmul(ps[:, n:2 * n], ones_b[:], sel_b[:], start=True, stop=True).then_inc(misc_ps, 1)

            def project(rd, name):
                i, item, ps = rd.i + 1, rd.item(name), misc_bank[rd.bank(name)]
                b, g = i // NKV, i % NKV
                if not (rd.prologue and item <= 2):
                    pe.wait_ge(misc_free, item - 2)
                tokens = [t[:, bass.ds(b * S, TOK + S)] for t in xnT]
                if name == "k":
                    chunk, w = NKV * DH, [t[:, bass.ds(g * DH, NKV * DH + DH)] for t in wkv_s]
                else:
                    chunk, w = GH * DH, [t[:, bass.ds(g * (KC * GH * DH) + int(name[1]) * DH, GH * DH + DH)] for t in wq_s]
                for c in range(KC):
                    for n, (a, m) in enumerate(PASSES):
                        ins = pe.matmul(ps[:], w[a][:, c * chunk:c * chunk + DH], tokens[m][:, c * TOK:c * TOK + S],
                                        start=(c == 0 and n == 0), stop=(c == KC - 1 and n == 2))
                ins.then_inc(misc_ps, 1)

            def project_values(rd):
                i, item, ps = rd.i, rd.item("v"), misc_bank[rd.bank("v")]
                b, g = i // NKV, i % NKV
                pe.wait_ge(misc_free, item - 2)
                chunk = NKV * DH
                tokens = [t[:, bass.ds(b * S, TOK + S)] for t in xnT]
                w = [t[:, bass.ds(KC * chunk + g * DH, chunk + DH)] for t in wkv_s]
                for q in range(QT):
                    for c in range(KC):
                        for n, (a, m) in enumerate(PASSES):
                            ins = pe.matmul(ps[:, q * DH:(q + 1) * DH], tokens[a][:, c * TOK + q * P:c * TOK + (q + 1) * P],
                                            w[m][:, c * chunk:c * chunk + DH],
                                            start=(c == 0 and n == 0), stop=(c == KC - 1 and n == 2))
                ins.then_inc(misc_ps, 1)

            def score(h, j, queries, keys, reuse):
                pe.wait_ge(rot_lo, queries)
                if keys is not None:
                    pe.wait_ge(rot_lo, keys)
                for u, unit in enumerate(SCORE_UNITS):
                    if reuse:
                        pe.wait_ge(exped, h * 3 + u - 2)
                    for qt, col in unit:
                        n_k = (qt + 1) * P
                        for n, (a, m) in enumerate(PASSES):
                            ins = pe.matmul(score_bank[u][:, col:col + n_k], qT[a][:, j * S + qt * P:j * S + (qt + 1) * P], kT[m][:, 0:n_k],
                                            start=(n == 0), stop=(n == 2))
                    ins.then_inc(scores, 1)

            def transpose_probs(h, j, units, first):
                for u in units:
                    if u == 0:
                        pe.wait_ge(normed, h + 1)
                    if not first or j > 0 or u == 2:
                        pe.wait_ge(pt_lo, h * 3 + u - 1)
                    for kt, col in PT_UNITS[u]:
                        for qt in range(kt, QT):
                            ins = pe.transpose(pt_bank[(3 * j + u) % 2][:, col + (qt - kt) * P:col + (qt - kt + 1) * P],
                                               probs[j % 2][:, P_AT[qt] + kt * P:P_AT[qt] + (kt + 1) * P], ident_f[:])
                    ins.then_inc(pt_ps, 1)

            def weigh_values(rd, j):
                h = rd.head(j)
                if j == 0:
                    pe.wait_ge(misc_free, rd.item("v"))
                if j > 0 or not rd.first:
                    pe.wait_ge(o_lo, h)
                for kt in (0, 1, 3, 2):
                    n_q = (QT - kt) * P
                    if kt != 3:
                        pe.wait_ge(pt_lo, h * 3 + kt + 1)
                    for n, (a, m) in enumerate(PASSES):
                        ins = pe.matmul(o_bank[:, kt * P:S], v_s[a][:, kt * DH:(kt + 1) * DH], pT[j % 2][m][:, PT_AT[kt]:PT_AT[kt] + n_q],
                                        start=(kt == 0 and n == 0), stop=(kt == 2 and n == 2))
                ins.then_inc(pv, 1)

            def project_out(rd, q):
                i, item, ps = rd.i - 1, rd.item(f"o{q}"), misc_bank[rd.bank(f"o{q}")]
                pe.wait_ge(o_lo, rd.i * GH - 1 if rd is EPILOGUE else rd.i * GH)
                pe.wait_ge(misc_free, item - 2)
                heads = [t[:, bass.ds((i % 2) * (GH * S), GH * S)] for t in oT]
                w = [t[:, bass.ds((i % NKV) * (GH * D), GH * D)] for t in wo_s]
                for j in range(GH):
                    if rd is EPILOGUE and j == GH - 1:
                        pe.wait_ge(o_lo, rd.i * GH)
                    for n, (a, m) in enumerate(PASSES):
                        ins = pe.matmul(ps[:, 0:D], heads[a][:, j * S + q * P:j * S + (q + 1) * P], w[m][:, j * D:(j + 1) * D],
                                        start=(j == 0 and n == 0), stop=(j == GH - 1 and n == 2))
                ins.then_inc(misc_ps, 1)

            pe.wait_ge(w_lo, 2)
            pe.wait_ge(xnT_lo, KC)
            project(PROLOGUE, "q0")
            project(PROLOGUE, "k")
            project(PROLOGUE, "q1")
            project(PROLOGUE, "q2")
            pe.wait_ge(const_cast, 4)
            score(0, 0, PROLOGUE.rot("q0"), PROLOGUE.rot("k"), False)
            project(PROLOGUE, "q3")

            def round_(rd):
                queries = [rd.i * 5 + n for n in (1, PROLOGUE.rot("q1") if rd.first else 2, 4, 5)]
                for j in range(GH - 1):
                    h = rd.head(j)
                    score(h + 1, j + 1, queries[j + 1], None, True)
                    if j == 0:
                        if rd.first:
                            pe.wait_ge(w_lo, W_FIRST)
                        if not rd.last:
                            project(rd, "q0")
                        transpose_probs(h, j, (0, 1), rd.first)
                        if not rd.first:
                            weigh_values(rd, -1)
                        project_values(rd)
                        transpose_probs(h, j, (2,), rd.first)
                    else:
                        transpose_probs(h, j, (0, 1), rd.first)
                        if rd.first:
                            transpose_x_items(rd, X_BEFORE[j])
                        if not rd.last:
                            project(rd, ("q0", "q1", "k")[j])
                        if not rd.first:
                            project_out(rd, j - 1)
                        transpose_probs(h, j, (2,), rd.first)
                        weigh_values(rd, j - 1)
                        if rd.second and j == 2:
                            rank(rd)
                    if rd.first:
                        transpose_x_items(rd, X_AFTER[j])
                if not rd.last:
                    project(rd, "q2")
                if rd.first:
                    transpose_x_items(rd, X_AFTER[GH - 1])
                else:
                    project_out(rd, 2)
                transpose_probs(rd.head(3), 3, (0, 1), rd.first)
                weigh_values(rd, 2)
                if not rd.last:
                    score(rd.head(GH), 0, rd.rot("q0"), rd.rot("k"), True)
                    project(rd, "q3")
                transpose_probs(rd.head(3), 3, (2,), rd.first)
                if rd.first:
                    router(rd)
                else:
                    project_out(rd, 3)

            round_(Round(0, "first"))
            pe.wait_ge(w_lo, W_FIRST + 2)
            round_(Round(1, "second"))
            pe.wait_ge(w_lo, W_FIRST + 4)
            round_(Round(2, "third"))
            pe.wait_ge(w_lo, N_CHUNKS)
            with pe.Fori(3, NG - 1) as i:
                round_(Round(i, "loop"))
            round_(Round(NG - 1, "last"))
            weigh_values(EPILOGUE, -1)
            for q in range(QT):
                project_out(EPILOGUE, q)

            experts = [None]

            def load_experts(st):
                experts[0] = pe.value_load(group_u[0:1, bass.ds(st.tile() // GROUP, 1)], min_val=0, max_val=E_ROUTED ** (GROUP + LAG) - 1)

            def weights(st, back=0):
                if st.routed(back):
                    k = st.ring(GROUP, back)
                    before = st.routed(st.ring(GROUP)) and k > st.ring(GROUP)
                    e = experts[0] // E_ROUTED ** (k + LAG - (GROUP if before else 0)) % E_ROUTED
                    return [w[:, bass.ds(e * WE, WE)] for w in expert_s]
                return shared_s

            def step(st):
                n = st.n
                if st.like == SH_FIRST:
                    pe.wait_ge(tiles_ready, 1)
                if st.ring(GROUP) == 0 and st.routed():
                    load_experts(st)
                if st.gu:
                    gu = gu_bank[st.ring(2)][:, 0:GU]
                    if st.like == 0:
                        pe.wait_ge(shared_w, 2)
                    if st.like >= 2:
                        pe.wait_ge(hidden, n - 1)
                    if st.routed():
                        if st.like == SH_FIRST:
                            pe.wait_ge(even_lo, E_ROUTED // 2)
                            pe.wait_ge(odd_lo, E_ROUTED // 2)
                        pe.wait_ge(xT_lo, st.tile() + 1)
                        tokens, chunk = xT[st.ring(2)], P
                    else:
                        tokens, chunk = [w[:, st.tile() * P:TOK + (st.tile() + 1) * P] for w in xnT], TOK
                    w, half = weights(st), 0 if st.routed() else st.like % E_SHARED
                    for c in range(KC):
                        for p, (a, b) in enumerate(PASSES):
                            ins = pe.matmul(gu, tokens[a][:, c * chunk:c * chunk + P], w[b][:, half * WG + c * GU:half * WG + (c + 1) * GU],
                                            start=(c == 0 and p == 0), stop=(c == KC - 1 and p == 2))
                    ins.then_inc(gu_ps, 1)
                if st.t:
                    pe.wait_ge(hidden, n)
                    if st.like > 2 * E_SHARED:
                        pe.wait_ge(hT_lo, st.layers(1) - 2)
                    at = (st.ring(4, 1) if st.routed(1) else st.pair(1)) * INTER
                    for c, rows_ in enumerate((HC, HC) if st.routed(1) else SHARED_ROWS):
                        ins = pe.transpose(hT_bank[st.parity(1)][0:rows_, c * P:(c + 1) * P], hid[:, at:at + rows_], ident_f[:])
                        at += rows_
                    ins.then_inc(hT_ps, 1)
                if st.rows:
                    m = st.tile(-2)
                    if st.like + 2 == SH_FIRST:
                        pe.wait_ge(misc_free, ATTENTION_ITEMS)
                    pe.wait_ge(xs_in[st.ring(4, -2)], (m - st.ring(4, -2)) * 4 + 16)
                    if st.like + 2 >= SH_FIRST + 2:
                        pe.wait_ge(xT_lo, m - 1)
                    for c in range(KC):
                        ins = pe.transpose(xT_bank[st.ring(2)][:, c * P:(c + 1) * P], xs[:, st.ring(4, -2), c * P:(c + 1) * P], ident_f[:])
                    ins.then_inc(xT_ps, 1)
                if st.y:
                    w = weights(st, LAG)
                    if st.routed(LAG) and not st.routed(LAG + 2):
                        pe.wait_ge(y_done, SH_TILES - 1 + st.like - LAG - SH_FIRST)
                    elif st.routed(LAG):
                        pe.wait_ge(ys_ready, st.tile(LAG) - 1)
                    elif ROUTED_END <= st.like - LAG < ROUTED_END + 2 * E_SHARED:
                        pe.wait_ge(ys_ready, R_TILES - 1 + st.tile(LAG) - SH_TILES)
                    elif st.tile(LAG) >= 2:
                        pe.wait_ge(y_done, st.tile(LAG) - 1)
                    at = (st.ring(4, LAG) if st.routed(LAG) else st.pair(LAG)) * 2 * P
                    chunks, down = ((HC, HC), WG) if st.routed(LAG) else (SHARED_ROWS, SHARED_WG)
                    pe.wait_ge(hT_hi, st.layers(LAG))
                    for p, (a, b) in enumerate(PASSES):
                        if p == 2:
                            pe.wait_ge(hT_lo, st.layers(LAG))
                        for c, rows_ in enumerate(chunks):
                            ins = pe.matmul(y_bank[st.parity(LAG)][:, 0:D], hT_flat[a][0:rows_, at + c * P:at + (c + 1) * P],
                                            w[b][0:rows_, down + c * D:down + (c + 1) * D],
                                            start=(c == 0 and p == 0), stop=(c == len(chunks) - 1 and p == 2))
                    ins.then_inc(down_ps, 1)

            ffn_steps(pe, step)


def kernel(**inputs):
    import numpy as np
    import concourse.bacc as bacc
    from concourse.bass_utils import run_bass_kernel_spmd

    pos = np.arange(S, dtype=np.float32)
    half = DH // 2
    inv_freq = (1.0 / 10000.0 ** (np.arange(half, dtype=np.float32) / np.float32(half))).astype(np.float32)
    freqs = np.outer(pos, inv_freq).astype(np.float32)
    cos = np.cos(np.concatenate([freqs, freqs], -1)).astype(np.float64)
    sin = np.sin(np.concatenate([freqs, freqs], -1)).astype(np.float64)
    scale = (pos.astype(np.float64) + 32.0) / 64.0
    xs = np.stack([np.repeat(scale[:, None], half, 1), np.repeat(1.0 / scale[:, None], half, 1)], -1).reshape(S, DH)
    sgn = np.concatenate([-np.ones(half), np.ones(half)])
    qs, ks = xs / np.sqrt(DH), 1.0 / xs
    tables = [cos * qs, np.roll(sin * sgn * qs, -half, 1), cos * ks, np.roll(sin * sgn * ks, -half, 1)]
    rope = np.ascontiguousarray(np.stack([t.T for t in tables]).astype(np.float32))

    token = np.arange(NT)[None, None] * P + np.arange(P)[:, None, None]
    rows = (TOP_K * token + np.arange(TOP_K)[None, :, None]).reshape(P, TOP_K * NT)
    empty = TOP_K * TOK + np.arange(R_TILES // FILLS)[None] * P + np.arange(P)[:, None]
    rows = np.concatenate([rows, empty], 1).astype(np.float32)

    arrays = {
        "x": inputs["L0_attn_x"], "wq": inputs["L0_attn_Wq"], "wk": inputs["L0_attn_Wk"], "wv": inputs["L0_attn_Wv"],
        "wo": inputs["L0_attn_Wo"], "gate_t": np.asarray(inputs["L0_ffn_gate_w"]).T, "w_gate_up": inputs["L0_ffn_w_gate_up"],
        "w_down": inputs["L0_ffn_w_down"], "shared_gu": inputs["L0_ffn_shared_gate_up"], "shared_down": inputs["L0_ffn_shared_down"],
        "rope": rope, "ident": np.eye(P, dtype=np.float32),
        "mask": np.where(np.tril(np.ones((P, P), bool)), 0.0, -1e30).astype(np.float32),
        "iota": np.tile(np.arange(R_TILES, dtype=np.float32), (P, 1)), "tri": np.triu(np.ones((P, P), np.float32), 1),
        "rows": rows, "digits": (float(E_ROUTED) ** (np.arange(R_TILES) % GROUP + LAG)).astype(np.float32)[None],
    }
    arrays = {n: np.ascontiguousarray(a) for n, a in arrays.items()}
    nc = bacc.Bacc("TRN2", target_bir_lowering=False, num_devices=1)
    aps = [nc.dram_tensor(n, a.shape, mybir.dt.from_np(a.dtype), kind="ExternalInput").ap() for n, a in arrays.items()]
    aps.append(nc.dram_tensor("out", (B, S, D), F32, kind="ExternalOutput").ap())
    build(nc, *aps)
    return run_bass_kernel_spmd(nc, [arrays], core_ids=[0]).results[0]["out"]
```
